# Optimizing a Trainium2 kernel written in Bass

```python
import numpy as np
import jax
import jax.numpy as jnp

def _softmax(x, axis=-1):
    return jax.nn.softmax(x, axis=axis)

def _gelu(x):
    return jax.nn.gelu(x, approximate=True)

def _silu(x):
    return jax.nn.silu(x)

def _sigmoid(x):
    return jax.nn.sigmoid(x)

def _layernorm(x, axis=-1, eps=1e-05):
    m = jnp.mean(x, axis=axis, keepdims=True)
    v = jnp.var(x, axis=axis, keepdims=True)
    return (x - m) / jnp.sqrt(v + eps)

def _scatter_add(tgt, idx, src, axis=0):
    return tgt.at[idx].add(src)

def _segment_sum(src, seg, n):
    return jax.ops.segment_sum(src, seg, n)
kernel_name = 'mk_flamingo_gated_d1_seqx_r8_892359'

def setup_inputs(seed: int=0):
    np.random.seed(seed)
    _w = jnp.asarray

    def _rec_inputs():
        import jax
        import jax.numpy as jnp
        _rk = jax.random.key(seed)
        x = 0.5 + 0.2887 * jax.random.normal(jax.random.fold_in(_rk, 1), (4, 256, 256), jnp.float32)
        _lenS = 256 - jax.random.randint(jax.random.fold_in(_rk, 7), (4,), 0, max(1, 256 // 4) + 1, jnp.int32)
        _lenS2 = 256 - jax.random.randint(jax.random.fold_in(_rk, 8), (4,), 0, max(1, 256 // 4) + 1, jnp.int32)
        _ctx_512P = jax.random.normal(jax.random.fold_in(_rk, 11), (4, 16, 64), jnp.float32)
        _ctx_512c = jax.random.dirichlet(jax.random.fold_in(_rk, 511), 0.3 * jnp.ones((16,), jnp.float32), (4, 256))
        _ctx_512t = jnp.einsum('bsk,bkd->bsd', _ctx_512c, _ctx_512P)
        _ctx_512t = _ctx_512t * jax.lax.rsqrt(jnp.mean(jnp.square(_ctx_512t)) + 1e-12) * 0.953939
        ctx_512 = 7.22013e-05 + 1.00017 * (_ctx_512t + 0.3 * jax.random.normal(jax.random.fold_in(_rk, 611), (4, 256, 64), jnp.float32))
        _g = jax.random.normal(jax.random.fold_in(_rk, 9001), (2, 1), jnp.float32)
        _g = jnp.sign(_g) * jnp.maximum(jnp.abs(_g), 1.0) + (_g == 0) * 1.0
        g_xattn = _g[0]
        g_ffn = _g[1]
        return (x, ctx_512, g_xattn, g_ffn)
    x, ctx_512, g_xattn, g_ffn = _rec_inputs()

    def _L0_xattn_setup():
        import jax, jax.numpy as jnp
        import numpy as np
        P_ASEM = 0.6
        key = jax.random.key(seed)
        k1, k2, k3 = jax.random.split(key, 3)
        B, N, D = (8, 256, 64)
        x = jax.random.normal(k1, (B, N, D), dtype=jnp.float32)
        adj = jax.random.uniform(k2, (B, N, N), dtype=jnp.float32)
        bound = 1.0 / np.sqrt(2 * D)
        W = jax.random.uniform(k3, (1, 2 * D), dtype=jnp.float32, minval=-bound, maxval=bound)
        b = jnp.zeros((1,), dtype=jnp.float32)
        return {'x': x, 'adj': adj, 'W': W, 'b': b}
    _L0_xattn_all = _L0_xattn_setup()
    _L0_xattn_in = {k: v for k, v in _L0_xattn_all.items() if k in ('W', 'b')}
    del _L0_xattn_all

    def _L0_ffn_setup():
        import jax, jax.numpy as jnp
        import numpy as np
        H = 256
        M = 176
        E = 32
        TOPK = 6
        G = 8
        TOPK_G = 4
        SH = 2
        B, S = (1, 128)
        key = jax.random.key(seed)
        ks = jax.random.split(key, 9)
        sc = 0.02
        return {'x': jax.random.normal(ks[0], (B, S, H), dtype=jnp.float32), 'w_router': jax.random.normal(ks[1], (H, E), dtype=jnp.float32) * sc, 'corr_bias': jax.random.normal(ks[2], (E,), dtype=jnp.float32) * 0.1, 'gate_w': jax.random.normal(ks[3], (E, H, M), dtype=jnp.float32) * sc, 'up_w': jax.random.normal(ks[4], (E, H, M), dtype=jnp.float32) * sc, 'down_w': jax.random.normal(ks[5], (E, M, H), dtype=jnp.float32) * sc, 'sh_gate_w': jax.random.normal(ks[6], (H, M * SH), dtype=jnp.float32) * sc, 'sh_up_w': jax.random.normal(ks[7], (H, M * SH), dtype=jnp.float32) * sc, 'sh_down_w': jax.random.normal(ks[8], (M * SH, H), dtype=jnp.float32) * sc}
    _L0_ffn_all = _L0_ffn_setup()
    _L0_ffn_in = {k: v for k, v in _L0_ffn_all.items() if k in ('w_router', 'corr_bias', 'gate_w', 'up_w', 'down_w', 'sh_gate_w', 'sh_up_w', 'sh_down_w')}
    del _L0_ffn_all
    return {'x': x, 'ctx_512': ctx_512, 'g_xattn': g_xattn, 'g_ffn': g_ffn, 'L0_xattn_W': _L0_xattn_in['W'], 'L0_xattn_b': _L0_xattn_in['b'], 'L0_ffn_w_router': _L0_ffn_in['w_router'], 'L0_ffn_corr_bias': _L0_ffn_in['corr_bias'], 'L0_ffn_gate_w': _L0_ffn_in['gate_w'], 'L0_ffn_up_w': _L0_ffn_in['up_w'], 'L0_ffn_down_w': _L0_ffn_in['down_w'], 'L0_ffn_sh_gate_w': _L0_ffn_in['sh_gate_w'], 'L0_ffn_sh_up_w': _L0_ffn_in['sh_up_w'], 'L0_ffn_sh_down_w': _L0_ffn_in['sh_down_w']}

def reference(x, ctx_512, g_xattn, g_ffn, L0_xattn_W, L0_xattn_b, L0_ffn_w_router, L0_ffn_corr_bias, L0_ffn_gate_w, L0_ffn_up_w, L0_ffn_down_w, L0_ffn_sh_gate_w, L0_ffn_sh_up_w, L0_ffn_sh_down_w):
    import jax
    import jax.numpy as jnp

    def _L0_xattn_ref(x, adj, W, b):
        import jax, jax.numpy as jnp
        import numpy as np
        P_ASEM = 0.6
        D = x.shape[-1]
        Wi = W[:, :D]
        Wj = W[:, D:]
        si = jnp.einsum('bnd,d->bn', x, Wi[0])
        sj = jnp.einsum('bnd,d->bn', x, Wj[0])
        xij = jax.nn.sigmoid(si[:, :, None] + sj[:, None, :] + b[0])
        return P_ASEM * xij + (1.0 - P_ASEM) * adj

    def _L0_ffn_ref(x, w_router, corr_bias, gate_w, up_w, down_w, sh_gate_w, sh_up_w, sh_down_w):
        import jax, jax.numpy as jnp
        import numpy as np
        H = 256
        M = 176
        E = 32
        TOPK = 6
        G = 8
        TOPK_G = 4
        SH = 2
        B, S = (1, 128)
        b, s, h = x.shape
        xf = x.reshape(-1, h)
        T = xf.shape[0]
        logits = xf @ w_router
        scores = jax.nn.sigmoid(logits)
        sfc = scores + corr_bias
        grp = sfc.reshape(T, G, E // G)
        top2, _ = jax.lax.top_k(grp, 2)
        group_scores = top2.sum(-1)
        _, gidx = jax.lax.top_k(group_scores, TOPK_G)
        group_mask = jax.nn.one_hot(gidx, G, dtype=jnp.float32).sum(axis=1) > 0
        score_mask = jnp.repeat(group_mask, E // G, axis=1)
        masked = jnp.where(score_mask, sfc, -jnp.inf)
        _, topk_idx = jax.lax.top_k(masked, TOPK)
        topk_w = jnp.take_along_axis(scores, topk_idx, axis=1)
        combine = jnp.zeros((T, E), dtype=x.dtype).at[jnp.arange(T)[:, None], topk_idx].add(topk_w)
        g = jnp.einsum('th,ehm->etm', xf, gate_w)
        u = jnp.einsum('th,ehm->etm', xf, up_w)
        eo = jnp.einsum('etm,emh->eth', jax.nn.silu(g) * u, down_w)
        routed = jnp.einsum('te,eth->th', combine, eo)
        shared = jax.nn.silu(xf @ sh_gate_w) * (xf @ sh_up_w) @ sh_down_w
        return (routed + shared).reshape(b, s, h)
    x = x + jnp.tanh(g_xattn[0]) * _L0_xattn_ref(ctx_512, _layernorm(x, axis=-1), L0_xattn_W, L0_xattn_b)
    x = x + jnp.tanh(g_ffn[0]) * _L0_ffn_ref(_layernorm(x, axis=-1), L0_ffn_w_router, L0_ffn_corr_bias, L0_ffn_gate_w, L0_ffn_up_w, L0_ffn_down_w, L0_ffn_sh_gate_w, L0_ffn_sh_up_w, L0_ffn_sh_down_w)
    return x

_drawn_inputs = setup_inputs


def setup_inputs(seed=0):
    import zlib

    import numpy as np

    out = dict(_drawn_inputs(seed))
    spreads = {}
    factors = {'L0_ffn_w_router': 4.16,
     'L0_ffn_corr_bias': 3.511,
     'L0_ffn_gate_w': 2.938,
     'L0_ffn_up_w': 2.907,
     'L0_ffn_down_w': 2.915,
     'L0_ffn_sh_gate_w': 2.894,
     'L0_ffn_sh_up_w': 2.829,
     'L0_ffn_sh_down_w': 2.845}
    for name, (base, spread) in spreads.items():
        noise = np.random.default_rng([zlib.crc32(name.encode()), seed]).standard_normal(out[name].shape)
        drawn = base * np.exp(spread * noise) if base else spread * noise
        out[name] = jnp.asarray(drawn.astype(out[name].dtype))
    for name, factor in factors.items():
        out[name] = (out[name] * factor).astype(out[name].dtype)
    return out
```

```python
from contextlib import ExitStack

import concourse.bass as bass
from concourse import mybir

F32 = mybir.dt.float32
BF16 = mybir.dt.bfloat16
I32 = mybir.dt.int32
ALU = mybir.AluOpType
ACT = mybir.ActivationFunctionType

P = 128
P_ASEM = 0.6
EPS = 1e-5
TOPK = 6
GROUPS = 8
TOPK_GROUPS = 4
RING = 4
ABSENT = -3.0e38
CHOSEN = 3.0e38
BARRED = -1.0e30


def gated_xattn_moe(nc, x, ctx, g_xattn, g_ffn, w_adj, b_adj, w_router, corr_bias, gate_w, up_w, down_w,
                    sh_gate_w, sh_up_w, sh_down_w, out):
    B, N, H = x.shape
    D = ctx.shape[2]
    E, _, M = gate_w.shape
    T = B * N
    J = T // P
    HALVES = N // P
    K = H // P
    M2 = M - P
    SH = sh_gate_w.shape[1] // M
    PER = E // GROUPS
    PAIRS = T * TOPK
    TILES = (PAIRS - E) // P + E
    TILES += -TILES % RING
    ROW = H + E
    UNITS = J * SH

    with ExitStack() as stack:
        def sb(name, shape, dt=F32):
            return stack.enter_context(nc.sbuf_tensor(name, shape, dt))

        def bank(name):
            return stack.enter_context(nc.psum_tensor(name, [P, 512], F32))

        def sem(name):
            return stack.enter_context(nc.semaphore(name))

        rows_dram = nc.dram_tensor("rows_dram", [T + P, ROW], F32, kind="Internal").ap()
        slots_dram = nc.dram_tensor("slots_dram", [P * TILES, 1], I32, kind="Internal").ap()
        sums_dram = [nc.dram_tensor(f"sum{i}_dram", [T + P, H], F32, kind="Internal").ap() for i in range(2)]

        wgu = sb("wgu", [P, E, K, 2 * M])
        wd0 = sb("wd0", [P, E, H])
        wd1 = sb("wd1", [M2, E, H])
        sgu = sb("sgu", [P, SH, K, 2 * M])
        sd0 = sb("sd0", [P, SH, H])
        sd1 = sb("sd1", [M2, SH, H])
        xs = sb("xs", [P, J, H])
        xn = sb("xn", [P, J, H])
        xnT = sb("xnT", [P, K, T])
        ctxT = xnT[0:D, 0, :]
        ident = sb("ident", [P, P])
        before = sb("before", [P, P], BF16)
        ones = sb("ones", [P, P], BF16)
        zeros = sb("zeros", [P, ROW])
        pad_ids = sb("pad_ids", [P, TILES], I32)
        tok_ids = sb("tok_ids", [P, J], I32)
        part_i = sb("part_i", [P, 1], I32)
        part_f = sb("part_f", [P, 1])
        wij = sb("wij", [D, 2])
        wj_wide = sb("wj_wide", [D, P])
        badj = sb("badj", [P, 1])
        gates = sb("gates", [P, 2])
        tg = sb("tg", [P, 2])
        kx = sb("kx", [P, 2])
        cb = sb("cb", [P, E])
        wr = sb("wr", [P, K, E])
        stats = sb("stats", [P, J, 6])
        mv = sb("mv", [P, J, 2])
        rstd = sb("rstd", [P, J])
        power = sb("power", [P, J])
        xa = sb("xa", [P, J])
        xc = sb("xc", [P, J])
        sib = sb("sib", [P, J])
        scores = sb("scores", [P, J, E])
        gkey = sb("gkey", [P, J, GROUPS + 8 - TOPK_GROUPS])
        gmark = sb("gmark", [P, J, GROUPS + 8 - TOPK_GROUPS])
        best = sb("best", [P, J, 8])
        key = sb("key", [P, J, E + 8 - TOPK])
        mark = sb("mark", [P, J, E + 8 - TOPK])
        chosen = sb("chosen", [P, J, E])
        chosen_b = sb("chosen_b", [P, J, E], BF16)
        comb = sb("comb", [P, J, E])
        cnt_i = sb("cnt_i", [P, 2, E], I32)
        ntile = sb("ntile", [P, E])
        tend = sb("tend", [P, E])
        tbase = sb("tbase", [P, E])
        zero_e = sb("zero_e", [P, E])
        slot_i = sb("slot_i", [P, J, 8], I32)
        past = sb("past", [P, E])
        tile_e = sb("tile_e", [P, 1])
        experts = sb("experts", [1, P], I32)
        slot_ids = sb("slot_ids", [P, TILES], I32)
        idx = sb("idx", [P, 2 * RING], I32)
        wt = sb("wt", [P, RING])
        sg = sb("sg", [P, 2, M])
        h = sb("h", [P, 2, M])
        hT = sb("hT", [P, 2, 2, P])
        y = sb("y", [P, RING, H])
        xn_flat = xn[:, :, :].rearrange("p j c -> p (j c)")
        xg = xn_flat[:, 0:RING * ROW].rearrange("p (s c) -> p s c", s=RING)
        xT = xn_flat[:, RING * ROW:RING * ROW + 2 * H].rearrange("p (s k t) -> p s k t", s=2, k=K)
        ctx_sb = y[:, 0:2, :].rearrange("p a (b d) -> p (a b) d", d=D)
        sig, mix = y[:, 0:2, :], y[:, 2:4, :]
        sfc = y[:, 0, :].rearrange("p (j e) -> p j e", e=E)
        pos_i, pos_t, pos_q = (y[:, i, :].bitcast(I32).rearrange("p (j e) -> p j e", e=E) for i in (1, 2, 3))
        pair = chosen[:, :, :].rearrange("p j e -> p (j e)").rearrange("p (a b) -> p a b", a=4)

        pX = [bank(f"pX{i}") for i in range(2)]
        pG = [bank(f"pG{i}") for i in range(2)]
        pH = [bank(f"pH{i}") for i in range(2)]
        pY = [bank(f"pY{i}") for i in range(2)]
        xn_banks = [pX[0], pX[1], pY[0], pY[1]]
        pos_bank, count_bank, expert_bank = pH[0], pG[0], pG[1]

        s_x, s_ctx, s_small, s_wr = sem("s_x"), sem("s_ctx"), sem("s_small"), sem("s_wr")
        s_shw, s_expw = sem("s_shw"), sem("s_expw")
        s_const, s_clear = sem("s_const"), sem("s_clear")
        s_dve = sem("s_dve")
        s_pool = sem("s_pool")
        s_tanh, s_ctxT, s_ctxTc, s_wide, s_sj, s_sib = (sem(n) for n in
            ("s_tanh", "s_ctxT", "s_ctxTc", "s_wide", "s_sj", "s_sib"))
        s_var, s_rstd, s_sig, s_x1 = sem("s_var"), sem("s_rstd"), sem("s_sig"), sem("s_x1")
        s_xn, s_xnT, s_xnTc, s_logit, s_score = (sem(n) for n in ("s_xn", "s_xnT", "s_xnTc", "s_logit", "s_score"))
        s_chosen, s_comb, s_pos, s_slot, s_tile_e, s_eT, s_experts = (sem(n) for n in
            ("s_chosen", "s_comb", "s_pos", "s_slot", "s_tile_e", "s_eT", "s_experts"))
        s_rows, s_pads, s_scat, s_ids = sem("s_rows"), sem("s_pads"), sem("s_scat"), sem("s_ids")
        s_gu, s_silu, s_h, s_hT, s_hTc, s_y, s_yc = (sem(n) for n in
            ("s_gu", "s_silu", "s_h", "s_hT", "s_hTc", "s_y", "s_yc"))
        s_xT, s_xTc, s_wt, s_idx = sem("s_xT"), sem("s_xTc"), sem("s_wt"), sem("s_idx")
        s_go = sem("s_go")
        s_gath = [sem(f"s_gath{i}") for i in range(RING)]
        s_add = [sem(f"s_add{i}") for i in range(RING)]
        s_sums, s_fin, s_out = sem("s_sums"), sem("s_fin"), sem("s_out")

        x_rows = x.rearrange("b (h p) c -> p (b h) c", p=P)
        out_rows = out.rearrange("b (h p) c -> p (b h) c", p=P)
        block = stack.enter_context(nc.Block())

        @block.sync
        def _(sp):
            sp.dma_start(ctx_sb, ctx.rearrange("b (h p) d -> p (b h) d", p=P)).then_inc(s_ctx, 16)
            for b in range(B):
                sp.dma_start(xs[:, b * HALVES:(b + 1) * HALVES, :],
                             x_rows[:, b * HALVES:(b + 1) * HALVES, :]).then_inc(s_x, 16)
            sp.dma_start(wr[:, :, :], w_router.rearrange("(k p) e -> p k e", p=P)).then_inc(s_wr, 16)
            for s in range(SH):
                cols = slice(s * M, (s + 1) * M)
                sp.dma_start(sgu[:, s, :, 0:M], sh_gate_w[:, cols].rearrange("(k p) m -> p k m", p=P)).then_inc(s_shw, 16)
                sp.dma_start(sgu[:, s, :, M:2 * M], sh_up_w[:, cols].rearrange("(k p) m -> p k m", p=P)).then_inc(s_shw, 16)
                sp.dma_start(sd0[:, s, :], sh_down_w[s * M:s * M + P, :]).then_inc(s_shw, 16)
                sp.dma_start(sd1[:, s, :], sh_down_w[s * M + P:(s + 1) * M, :]).then_inc(s_shw, 16)
            for e in range(E):
                sp.dma_start(wgu[:, e, :, 0:M], gate_w[e].rearrange("(k p) m -> p k m", p=P)).then_inc(s_expw, 16)
                sp.dma_start(wgu[:, e, :, M:2 * M], up_w[e].rearrange("(k p) m -> p k m", p=P)).then_inc(s_expw, 16)
            for e in range(0, E, 8):
                sp.dma_start(wd0[:, e:e + 8, :], down_w[e:e + 8, 0:P, :].rearrange("e p c -> p e c")).then_inc(s_expw, 16)
                sp.dma_start(wd1[:, e:e + 8, :], down_w[e:e + 8, P:M, :].rearrange("e p c -> p e c")).then_inc(s_expw, 16)
            for s in range(RING):
                sp.wait_ge(s_add[s], 16 * (TILES // RING))
            for i, into in enumerate((xn[:, :, :], xnT[:, :, :].rearrange("p k t -> p (k t)").rearrange("p (j c) -> p j c", c=H))):
                sp.dma_start(into, sums_dram[i][0:T, :].rearrange("(j p) c -> p j c", p=P)).then_inc(s_sums, 16)
            for b in range(B):
                sp.wait_ge(s_fin, b + 1)
                sp.dma_start(out_rows[:, b * HALVES:(b + 1) * HALVES, :],
                             xs[:, b * HALVES:(b + 1) * HALVES, :]).then_inc(s_out, 16)
            sp.wait_ge(s_out, 16 * B)

        @block.gpsimd
        def _(pool):
            made = [0]

            def chain(ins):
                made[0] += 1
                ins.then_inc(s_pool, 1)
                pool.wait_ge(s_pool, made[0])

            chain(pool.memset(ident[:, :], 0.0))
            pool.affine_select(out=ident[:, :], in_=ident[:, :], compare_op=ALU.not_equal, fill=1.0,
                               base=0, pattern=[[-1, P]], channel_multiplier=1).then_inc(s_const, 1)
            pool.memset(power[:, :], -0.5)
            pool.memset(ones[:, :], 1.0).then_inc(s_const, 1)
            chain(pool.memset(before[:, :], 0.0))
            chain(pool.affine_select(out=before[:, :], in_=before[:, :], compare_op=ALU.is_ge, fill=1.0,
                                     base=0, pattern=[[-1, P]], channel_multiplier=1))
            pool.iota(part_i[:, :], pattern=[[0, 1]], base=0, channel_multiplier=1).then_inc(s_const, 1)
            pool.iota(tok_ids[:, :], pattern=[[P, J]], base=0, channel_multiplier=1)
            chain(pool.iota(pad_ids[:, :], pattern=[[0, TILES]], base=T, channel_multiplier=1))
            pool.dma_start(slots_dram.rearrange("(p t) o -> p (t o)", p=P), pad_ids[:, :]).then_inc(s_pads, 16)
            chain(pool.memset(zeros[:, :], 0.0))
            pool.dma_start(rows_dram[T:T + P, :], zeros[:, :]).then_inc(s_clear, 16)
            for s in range(2):
                for j in range(J + 1):
                    pool.dma_start(sums_dram[s][j * P:(j + 1) * P, :], zeros[:, 0:H]).then_inc(s_clear, 16)
            for n in range(2):
                pool.wait_ge(s_var, n + 1)
                pool.tensor_tensor(out=rstd[:, :], in0=rstd[:, :], in1=power[:, :], op=ALU.pow).then_inc(s_rstd, 1)
            pool.wait_ge(s_pads, 16)
            pool.wait_ge(s_slot, 1)
            for j in range(J):
                for k in range(TOPK):
                    pool.indirect_dma_start(slots_dram[:, :], bass.IndirectOffsetOnAxis(ap=slot_i[:, j, k:k + 1], axis=0),
                                            tok_ids[:, j:j + 1], None).then_inc(s_scat, 16)
            pool.wait_ge(s_scat, 16 * J * TOPK)
            pool.dma_start(slot_ids[:, :], slots_dram.rearrange("(p t) o -> p (t o)", p=P)).then_inc(s_ids, 16)

            pool.wait_ge(s_rows, 16 * (B + 1))
            pool.wait_ge(s_clear, 16 * (1 + 2 * (J + 1)))
            pool.wait_ge(s_ids, 16)

            for s in range(RING):
                chain(pool.tensor_copy(idx[:, s:s + 1], slot_ids[:, s:s + 1]))
                pool.indirect_dma_start(xg[:, s, :], None, rows_dram[:, :],
                                        bass.IndirectOffsetOnAxis(ap=idx[:, s:s + 1], axis=0)).then_inc(s_gath[s], 16)

            def turn(i, s, more, first=False):
                t = i * RING + s
                if not first:
                    pool.wait_ge(s_add[s], 16 * i)
                pool.tensor_copy(idx[:, RING + s:RING + s + 1], slot_ids[:, bass.ds(t, 1)]).then_inc(s_idx, 1)
                if more:
                    pool.wait_ge(s_xT, t + 1)
                    pool.wait_ge(s_wt, t + 1)
                    pool.tensor_copy(idx[:, s:s + 1], slot_ids[:, bass.ds(t + RING, 1)]).then_inc(s_idx, 1)
                    pool.wait_ge(s_idx, 2 * t + 2)
                    pool.sem_inc(s_go, 1)
                    pool.indirect_dma_start(xg[:, s, :], None, rows_dram[:, :],
                                            bass.IndirectOffsetOnAxis(ap=idx[:, s:s + 1], axis=0)).then_inc(s_gath[s], 16)
                else:
                    pool.wait_ge(s_idx, 2 * (TILES - RING) + s + 1)
                pool.wait_ge(s_yc, t + (J + 1))
                if s >= 2:
                    pool.wait_ge(s_add[s - 2], i * 16 + 16)
                elif not first:
                    pool.wait_ge(s_add[s + 2], i * 16)
                pool.sem_inc(s_go, 1)
                pool.indirect_dma_start(sums_dram[s % 2][:, :],
                                        bass.IndirectOffsetOnAxis(ap=idx[:, RING + s:RING + s + 1], axis=0),
                                        y[:, s, :], None, compute_op=ALU.add).then_inc(s_add[s], 16)

            for s in range(RING):
                turn(0, s, True, first=True)
            with pool.Fori(1, TILES // RING - 1) as i:
                for s in range(RING):
                    turn(i, s, True)
            for s in range(RING):
                turn(TILES // RING - 1, s, False)

        @block.scalar
        def _(act):
            for c in range(2):
                act.dma_start(wij[:, c:c + 1], w_adj[:, c * D:(c + 1) * D].rearrange("o d -> d o")).then_inc(s_small, 16)
            act.dma_start(gates[:, 0:1], g_xattn.partition_broadcast(P)).then_inc(s_small, 16)
            act.dma_start(gates[:, 1:2], g_ffn.partition_broadcast(P)).then_inc(s_small, 16)
            act.dma_start(badj[:, :], b_adj.partition_broadcast(P)).then_inc(s_small, 16)
            act.dma_start(cb[:, :], corr_bias.partition_broadcast(P)).then_inc(s_small, 16)
            act.wait_ge(s_small, 96)
            nc.scalar.activation(tg[:, :], gates[:, :], ACT.Tanh).then_inc(s_tanh, 1)
            for c in range(2):
                act.wait_ge(s_ctxT, c + 1)
                nc.scalar.activation(ctxT[:, c * 512:(c + 1) * 512], pX[c][0:D, :], ACT.Copy).then_inc(s_ctxTc, 1)
            act.wait_ge(s_sib, 1)
            for j in range(J):
                b = j // HALVES
                if j == 0:
                    act.wait_ge(s_sj, B + 1)
                if j >= 2:
                    act.wait_ge(s_x1, j - 1)
                nc.scalar.activation(sig[:, j % 2, :], pG[b // 2][:, (b % 2) * N:(b % 2 + 1) * N], ACT.Sigmoid,
                                     bias=sib[:, j:j + 1]).then_inc(s_sig, 1)
            for j in range(0, J):
                if j % HALVES == HALVES - 1:
                    b = j // HALVES
                    act.wait_ge(s_xn, j + 1)
                    act.dma_start(rows_dram[0:T, 0:H].rearrange("(j p) c -> p j c", p=P)[:, b * HALVES:(b + 1) * HALVES, :],
                                  xn[:, b * HALVES:(b + 1) * HALVES, :]).then_inc(s_rows, 16)
                act.wait_ge(s_xnT, j + 1)
                nc.scalar.activation(xnT[:, :, j * P:(j + 1) * P],
                                     xn_banks[j % 4][:, 0:K * P].rearrange("p (k t) -> p k t", k=K),
                                     ACT.Copy).then_inc(s_xnTc, 1)
            act.wait_ge(s_logit, 1)
            nc.scalar.activation(scores[:, :, :].rearrange("p j e -> p (j e)"), pH[1][:, 0:J * E],
                                 ACT.Sigmoid).then_inc(s_score, 1)
            act.wait_ge(s_comb, 1)
            act.dma_start(rows_dram[0:T, H:ROW].rearrange("(j p) c -> p j c", p=P), comb[:, :, :]).then_inc(s_rows, 16)

            def silu(n, par):
                act.wait_ge(s_gu, n + 1)
                nc.scalar.activation(sg[:, par, :], pG[par][:, 0:M], ACT.Silu).then_inc(s_silu, 1)

            for n in range(UNITS):
                silu(n, n % 2)

            def copy_xT(t, par):
                act.wait_ge(s_xT, t + 1)
                nc.scalar.activation(xT[:, par, :, :].rearrange("p k t -> p (k t)"), pX[par][:, 0:K * P],
                                     ACT.Copy).then_inc(s_xTc, 1)

            def scale_y(t, s, reused, i):
                act.wait_ge(s_y, t + (J + 1))
                act.wait_ge(s_wt, t + 1)
                if reused:
                    act.wait_ge(s_add[s], i * 16)
                nc.scalar.activation(y[:, s, :], pY[s % 2][:, 0:H], ACT.Copy, scale=wt[:, s:s + 1]).then_inc(s_yc, 1)

            copy_xT(0, 0)
            silu(UNITS, 0)
            copy_xT(1, 1)

            def turn(i, s, left, reused=True):
                t = i * RING + s
                if left > 1:
                    silu(t + (UNITS + 1), (s + 1) % 2)
                if left > 2:
                    copy_xT(t + 2, s % 2)
                scale_y(t, s, reused, i)

            for s in range(RING):
                turn(0, s, TILES, reused=False)
            with act.Fori(1, TILES // RING - 1) as i:
                for s in range(RING):
                    turn(i, s, TILES)
            for s in range(RING):
                turn(TILES // RING - 1, s, RING - s)

        @block.tensor
        def _(pe):
            pe.wait_ge(s_const, 1)
            pe.wait_ge(s_ctx, 16)
            for j in range(J):
                ins = nc.tensor.transpose(pX[j // 4][0:D, (j % 4) * P:(j % 4 + 1) * P], ctx_sb[:, j, :], ident[:, :])
                if j % 4 == 3:
                    ins.then_inc(s_ctxT, 1)
            pe.wait_ge(s_small, 96)
            pe.wait_ge(s_wide, 1)
            pe.wait_ge(s_ctxTc, 2)
            for j in range(J):
                ins = nc.tensor.matmul(pH[0][:, j:j + 1], ctxT[:, j * P:(j + 1) * P], wij[:, 0:1], start=True, stop=True)
            ins.then_inc(s_sj, 1)
            for b in range(B):
                nc.tensor.matmul(pG[b // 2][:, (b % 2) * N:(b % 2 + 1) * N], wj_wide[:, :],
                                 ctxT[:, b * N:(b + 1) * N], start=True, stop=True).then_inc(s_sj, 1)
            for j in range(J):
                pe.wait_ge(s_xn, j + 1)
                if j >= 4:
                    pe.wait_ge(s_xnTc, j - 3)
                for k in range(K):
                    ins = nc.tensor.transpose(xn_banks[j % 4][:, k * P:(k + 1) * P], xn[:, j, k * P:(k + 1) * P], ident[:, :])
                ins.then_inc(s_xnT, 1)
            pe.wait_ge(s_wr, 16)
            for j in range(J):
                pe.wait_ge(s_xnTc, j + 1)
                for k in range(K):
                    ins = nc.tensor.matmul(pH[1][:, j * E:(j + 1) * E], xnT[:, k, j * P:(j + 1) * P], wr[:, k, :],
                                           start=(k == 0), stop=(k == K - 1))
            ins.then_inc(s_logit, 1)
            pe.wait_ge(s_chosen, 1)
            pe.wait_ge(s_const, 3)
            flat = chosen_b[:, :, :].rearrange("p j e -> p (j e)")
            nc.tensor.matmul(pos_bank[:, 0:J * E], before[:, :], flat, start=True, stop=False)
            for d in range(1, J):
                nc.tensor.matmul(pos_bank[:, d * E:J * E], ones[:, :], flat[:, 0:(J - d) * E], start=False, stop=(d == J - 1))
            for j in range(J):
                ins = nc.tensor.matmul(count_bank[:, 0:E], ones[:, :], chosen_b[:, j, :], start=(j == 0), stop=(j == J - 1))
            ins.then_inc(s_pos, 1)
            pe.wait_ge(s_tile_e, 1)
            nc.tensor.transpose(expert_bank[0:1, 0:P], tile_e[:, :], ident[:, :]).then_inc(s_eT, 1)
            pe.wait_ge(s_experts, 1)

            def gate_up(n, par, left, w):
                for k in range(K):
                    ins = nc.tensor.matmul(pG[par][:, 0:2 * M], left(k), w(k), start=(k == 0), stop=(k == K - 1))
                ins.then_inc(s_gu, 1)

            def turn_h(n, par):
                pe.wait_ge(s_h, n + 1)
                nc.tensor.transpose(pH[par][:, 0:P], h[:, par, 0:P], ident[:, :])
                nc.tensor.transpose(pH[par][0:M2, P:2 * P], h[:, par, P:M], ident[:, :]).then_inc(s_hT, 1)

            def down(n, par, bank, w0, w1, start, stop):
                pe.wait_ge(s_hTc, n + 1)
                nc.tensor.matmul(bank[:, 0:H], hT[:, par, 0, :], w0, start=start, stop=False)
                ins = nc.tensor.matmul(bank[:, 0:H], hT[0:M2, par, 1, :], w1, start=False, stop=stop)
                if stop:
                    ins.then_inc(s_y, 1)

            pe.wait_ge(s_shw, 16 * 4 * SH)

            def shared_gate_up(n):
                gate_up(n, n % 2, lambda k: xnT[:, k, (n // SH) * P:(n // SH + 1) * P], lambda k: sgu[:, n % SH, k, :])

            shared_gate_up(0)
            for n in range(UNITS):
                if n + 1 < UNITS:
                    shared_gate_up(n + 1)
                turn_h(n, n % 2)
                j, part = n // SH, n % SH
                if part == 0 and j >= 2:
                    pe.wait_ge(s_yc, j - 1)
                down(n, n % 2, pY[j % 2], sd0[:, part, :], sd1[:, part, :], part == 0, part == SH - 1)

            def transpose_x(s, rounds, par):
                pe.wait_ge(s_gath[s], 16 * rounds)
                for k in range(K):
                    ins = nc.tensor.transpose(pX[par][:, k * P:(k + 1) * P], xg[:, s, k * P:(k + 1) * P], ident[:, :])
                ins.then_inc(s_xT, 1)

            def routed_gate_up(t, par, e):
                pe.wait_ge(s_xTc, t + 1)
                gate_up(None, par, lambda k: xT[:, par, k, :], lambda k: wgu[:, bass.ds(e, 1), k, :])

            pe.wait_ge(s_expw, 16 * (2 * E + 2 * (E // 8)))

            def look_up(t):
                return pe.value_load(experts[0:1, bass.ds(t, 1)], min_val=0, max_val=E - 1)

            transpose_x(0, 1, 0)
            e_now = look_up(0)
            routed_gate_up(0, 0, e_now)
            transpose_x(1, 1, 1)

            def turn(i, s, left):
                t = i * RING + s
                e = look_up(t)
                turn_h(t + UNITS, s % 2)
                if left > 1:
                    routed_gate_up(t + 1, (s + 1) % 2, look_up(t + 1))
                if left > 2:
                    transpose_x((s + 2) % RING, i + (1 if s + 2 < RING else 2), s % 2)
                pe.wait_ge(s_yc, t + (J - 1))
                down(t + UNITS, s % 2, pY[s % 2], wd0[:, bass.ds(e, 1), :], wd1[:, bass.ds(e, 1), :], True, True)

            with pe.Fori(0, TILES // RING - 1) as i:
                for s in range(RING):
                    turn(i, s, TILES)
            for s in range(RING):
                turn(TILES // RING - 1, s, RING - s)

        @block.vector
        def _(dve):
            made = [0]
            V = nc.vector

            def link(ins):
                made[0] += 1
                ins.then_inc(s_dve, 1)
                dve.wait_ge(s_dve, made[0])

            dve.wait_ge(s_small, 96)
            V.tensor_copy(wj_wide[:, :], wij[:, 1:2].to_broadcast([D, P])).then_inc(s_wide, 1)
            V.memset(gkey[:, :, :], ABSENT)
            V.memset(key[:, :, :], ABSENT)
            V.memset(zero_e[:, :], 0.0)
            dve.wait_ge(s_tanh, 1)
            V.tensor_scalar(kx[:, 0:1], tg[:, 0:1], 1.0 - P_ASEM, None, ALU.mult)
            link(V.tensor_scalar(kx[:, 1:2], tg[:, 0:1], P_ASEM, None, ALU.mult))

            def norm_stats(n):
                for j in range(J):
                    if n == 0 and j % HALVES == 0:
                        dve.wait_ge(s_x, 16 * B)
                    link(V.bn_stats(stats[:, j, :], xs[:, j, :]))
                for j in range(J):
                    ins = V.bn_aggr(mv[:, j, :], stats[:, j, :])
                link(ins)
                V.tensor_scalar(rstd[:, :], mv[:, :, 1], EPS, None, ALU.add).then_inc(s_var, 1)
                dve.wait_ge(s_rstd, n + 1)

            norm_stats(0)
            link(V.tensor_scalar(xa[:, :], rstd[:, :], kx[:, 0:1], None, ALU.mult))
            link(V.scalar_tensor_tensor(xc[:, :], mv[:, :, 0], -1.0, xa[:, :], op0=ALU.mult, op1=ALU.mult))
            link(V.tensor_scalar(xa[:, :], xa[:, :], 1.0, None, ALU.add))
            dve.wait_ge(s_sj, 1)
            V.tensor_scalar(sib[:, :], pH[0][:, 0:J], badj[:, 0:1], None, ALU.add).then_inc(s_sib, 1)
            for j in range(J):
                link(V.tensor_scalar(mix[:, j % 2, :], xs[:, j, :], xa[:, j:j + 1], xc[:, j:j + 1], ALU.mult, ALU.add))
                dve.wait_ge(s_sig, j + 1)
                V.scalar_tensor_tensor(xs[:, j, :], sig[:, j % 2, :], kx[:, 1:2], mix[:, j % 2, :],
                                       op0=ALU.mult, op1=ALU.add).then_inc(s_x1, 1)
            dve.wait_ge(s_x1, J)
            norm_stats(1)
            for j in range(J):
                V.tensor_scalar(xn[:, j, :], xs[:, j, :], mv[:, j, 0:1], rstd[:, j:j + 1],
                                ALU.subtract, ALU.mult).then_inc(s_xn, 1)

            dve.wait_ge(s_score, 1)
            link(V.tensor_tensor(sfc[:, :, :], scores[:, :, :],
                                 cb[:, :].unsqueeze(1).to_broadcast([P, J, E]), ALU.add))
            four = sfc[:, :, :].rearrange("p j (g e) -> p (j g) e", e=PER)
            V.tensor_tensor(pair[:, 0, :], four[:, :, 0], four[:, :, 1], ALU.max)
            V.tensor_tensor(pair[:, 1, :], four[:, :, 0], four[:, :, 1], ALU.min)
            V.tensor_tensor(pair[:, 2, :], four[:, :, 2], four[:, :, 3], ALU.max)
            link(V.tensor_tensor(pair[:, 3, :], four[:, :, 2], four[:, :, 3], ALU.min))
            link(V.tensor_tensor(pair[:, 1, :], pair[:, 1, :], pair[:, 3, :], ALU.max))
            link(V.tensor_tensor(pair[:, 3, :], pair[:, 0, :], pair[:, 2, :], ALU.min))
            V.tensor_tensor(pair[:, 0, :], pair[:, 0, :], pair[:, 2, :], ALU.max)
            link(V.tensor_tensor(pair[:, 1, :], pair[:, 1, :], pair[:, 3, :], ALU.max))
            link(V.tensor_tensor(gkey[:, :, 0:GROUPS], pair[:, 0, :].rearrange("p (j g) -> p j g", g=GROUPS),
                                 pair[:, 1, :].rearrange("p (j g) -> p j g", g=GROUPS), ALU.add))

            def choose(marks, keys, n, top):
                for j in range(J):
                    ins = V.max(best[:, j, :], keys[:, j, 0:n])
                link(ins)
                link(V.memset(best[:, :, top:8], ABSENT))
                for j in range(J):
                    ins = V.match_replace(out=marks[:, j, :], in_to_replace=best[:, j, :], in_values=keys[:, j, :],
                                          imm_value=CHOSEN)
                link(ins)

            choose(gmark, gkey, GROUPS, TOPK_GROUPS)
            link(V.tensor_scalar(gmark[:, :, 0:GROUPS], gmark[:, :, 0:GROUPS], CHOSEN, BARRED, ALU.is_lt, ALU.mult))
            for e in range(PER):
                ins = V.tensor_tensor(key[:, :, 0:E].rearrange("p j (g e) -> p j g e", e=PER)[:, :, :, e],
                                      sfc[:, :, :].rearrange("p j (g e) -> p j g e", e=PER)[:, :, :, e],
                                      gmark[:, :, 0:GROUPS], ALU.add)
            link(ins)
            choose(mark, key, E, TOPK)
            V.tensor_scalar(chosen_b[:, :, :], mark[:, :, 0:E], CHOSEN, None, ALU.is_equal).then_inc(s_chosen, 1)
            link(V.tensor_scalar(chosen[:, :, :], mark[:, :, 0:E], CHOSEN, None, ALU.is_equal))
            V.scalar_tensor_tensor(comb[:, :, :], scores[:, :, :], tg[:, 1:2], chosen[:, :, :],
                                   op0=ALU.mult, op1=ALU.mult).then_inc(s_comb, 1)

            dve.wait_ge(s_pos, 1)
            link(V.tensor_scalar(cnt_i[:, 0, :], count_bank[:, 0:E], float(P - 1), None, ALU.add))
            link(V.tensor_scalar(cnt_i[:, 1, :], cnt_i[:, 0, :], 7, None, ALU.logical_shift_right))
            link(V.tensor_scalar(ntile[:, :], cnt_i[:, 1, :], 1.0, None, ALU.max))
            link(V.tensor_tensor_scan(tend[:, :], ntile[:, :], zero_e[:, :], 0.0, ALU.add, ALU.add))
            link(V.tensor_tensor(tbase[:, :], tend[:, :], ntile[:, :], ALU.subtract))
            link(V.tensor_copy(pos_i[:, :, :].rearrange("p j e -> p (j e)"), pos_bank[:, 0:J * E]))
            V.tensor_scalar(pos_t[:, :, :], pos_i[:, :, :], 7, None, ALU.logical_shift_right)
            link(V.tensor_scalar(pos_q[:, :, :], pos_i[:, :, :], P - 1, None, ALU.bitwise_and))
            link(V.scalar_tensor_tensor(mark[:, :, 0:E], pos_q[:, :, :], float(TILES), pos_t[:, :, :],
                                        op0=ALU.mult, op1=ALU.add))
            link(V.tensor_tensor(mark[:, :, 0:E], mark[:, :, 0:E], tbase[:, :].unsqueeze(1).to_broadcast([P, J, E]), ALU.add))
            link(V.scalar_tensor_tensor(mark[:, :, 0:E], mark[:, :, 0:E], 1.0, chosen[:, :, :], op0=ALU.add, op1=ALU.mult))
            for j in range(J):
                ins = V.max(best[:, j, :], mark[:, j, 0:E])
            link(ins)
            V.tensor_scalar(slot_i[:, :, :], best[:, :, :], -1.0, None, ALU.add).then_inc(s_slot, 1)
            dve.wait_ge(s_const, 3)
            link(V.tensor_copy(part_f[:, :], part_i[:, :]))
            link(V.tensor_scalar(past[:, :], tend[:, :], part_f[:, 0:1], None, ALU.is_le))
            link(V.reduce_sum(tile_e[:, :], past[:, :], axis=mybir.AxisListType.X))
            V.tensor_scalar(tile_e[:, :], tile_e[:, :], float(E - 1), None, ALU.min).then_inc(s_tile_e, 1)
            dve.wait_ge(s_eT, 1)
            V.tensor_copy(experts[0:1, :], expert_bank[0:1, 0:P]).then_inc(s_experts, 1)
            dve.wait_ge(s_experts, 1)

            def gate(n, par):
                dve.wait_ge(s_silu, n + 1)
                V.tensor_tensor(h[:, par, :], sg[:, par, :], pG[par][:, M:2 * M], ALU.mult).then_inc(s_h, 1)

            def copy_hT(n, par):
                dve.wait_ge(s_hT, n + 1)
                V.tensor_copy(hT[:, par, 0, :], pH[par][:, 0:P])
                V.tensor_copy(hT[0:M2, par, 1, :], pH[par][0:M2, P:2 * P]).then_inc(s_hTc, 1)

            gate(0, 0)
            for n in range(UNITS):
                if n + 1 < UNITS:
                    gate(n + 1, (n + 1) % 2)
                if n >= 2:
                    dve.wait_ge(s_y, n // SH - 1 if n % SH == 0 else (n - 1) // SH)
                copy_hT(n, n % 2)
                if n % SH == SH - 1:
                    j = n // SH
                    dve.wait_ge(s_y, j + 1)
                    V.scalar_tensor_tensor(xs[:, j, :], pY[j % 2][:, 0:H], tg[:, 1:2], xs[:, j, :],
                                           op0=ALU.mult, op1=ALU.add).then_inc(s_yc, 1)

            def copy_weight(t, s, rounds):
                e = dve.value_load(experts[0:1, bass.ds(t, 1)], min_val=0, max_val=E - 1)
                dve.wait_ge(s_gath[s], 16 * rounds)
                V.tensor_copy(wt[:, s:s + 1], xg[:, s, bass.ds(e + H, 1)]).then_inc(s_wt, 1)

            copy_weight(0, 0, 1)
            gate(UNITS, 0)
            copy_weight(1, 1, 1)

            def turn(i, s, left, first=False):
                t = i * RING + s
                if not first or s >= 2:
                    dve.wait_ge(s_y, t + (J - 1))
                copy_hT(t + UNITS, s % 2)
                if left > 1:
                    gate(t + (UNITS + 1), (s + 1) % 2)
                if left > 2:
                    if not first or s >= 2:
                        dve.wait_ge(s_yc, t + (J - 1))
                    copy_weight(t + 2, (s + 2) % RING, i + (1 if s + 2 < RING else 2))

            for s in range(RING):
                turn(0, s, TILES, first=True)
            with dve.Fori(1, TILES // RING - 1) as i:
                for s in range(RING):
                    turn(i, s, TILES)
            for s in range(RING):
                turn(TILES // RING - 1, s, RING - s)
            dve.wait_ge(s_sums, 32)
            dve.wait_ge(s_yc, J + TILES)
            second = xnT[:, :, :].rearrange("p k t -> p (k t)").rearrange("p (j c) -> p j c", c=H)
            for b in range(B):
                js = slice(b * HALVES, (b + 1) * HALVES)
                link(V.tensor_tensor(xn[:, js, :], xn[:, js, :], second[:, js, :], ALU.add))
                V.tensor_tensor(xs[:, js, :], xs[:, js, :], xn[:, js, :], ALU.add).then_inc(s_fin, 1)


_INS = ['x', 'ctx_512', 'g_xattn', 'g_ffn', 'L0_xattn_W', 'L0_xattn_b', 'L0_ffn_w_router', 'L0_ffn_corr_bias',
        'L0_ffn_gate_w', 'L0_ffn_up_w', 'L0_ffn_down_w', 'L0_ffn_sh_gate_w', 'L0_ffn_sh_up_w', 'L0_ffn_sh_down_w']
_OUTS = [((4, 256, 256), 'float32')]


def kernel(**inputs):
    import numpy as _np
    import concourse.bacc as _bacc
    from concourse import mybir as _mybir
    from concourse.bass_utils import run_bass_kernel_spmd as _run

    nc = _bacc.Bacc("TRN2", target_bir_lowering=False, num_devices=1)
    arrays, args = {}, []
    for name in _INS:
        a = _np.ascontiguousarray(inputs[name])
        arrays[f"in_{name}_dram"] = a
        args.append(nc.dram_tensor(f"in_{name}_dram", a.shape, _mybir.dt.from_np(a.dtype), kind="ExternalInput").ap())
    for i, (shape, dtype) in enumerate(_OUTS):
        dt = _mybir.dt.from_np(_np.dtype(dtype))
        args.append(nc.dram_tensor(f"out_{i}_dram", shape, dt, kind="ExternalOutput").ap())
    gated_xattn_moe(nc, *args)
    r = _run(nc, [arrays], core_ids=[0])
    got = tuple(r.results[0][f"out_{i}_dram"] for i in range(len(_OUTS)))
    return got[0]
```

```python
from contextlib import ExitStack

import concourse.bass as bass
from concourse import mybir

F32 = mybir.dt.float32
BF16 = mybir.dt.bfloat16
I32 = mybir.dt.int32
ALU = mybir.AluOpType
ACT = mybir.ActivationFunctionType

P = 128
P_ASEM = 0.6
EPS = 1e-5
TOPK = 6
GROUPS = 8
TOPK_GROUPS = 4
RING = 6
ABSENT = -3.0e38
CHOSEN = 3.0e38
BARRED = -1.0e30


def gated_xattn_moe(nc, x, ctx, g_xattn, g_ffn, w_adj, b_adj, w_router, corr_bias, gate_w, up_w, down_w,
                    sh_gate_w, sh_up_w, sh_down_w, out):
    B, N, H = x.shape
    D = ctx.shape[2]
    E, _, M = gate_w.shape
    T = B * N
    J = T // P
    HALVES = N // P
    K = H // P
    M2 = M - P
    SH = sh_gate_w.shape[1] // M
    PER = E // GROUPS
    PAIRS = T * TOPK
    TILES = (PAIRS - E) // P + E
    FULL, REST = TILES // RING, TILES % RING
    ROW = H + E + 1
    REGION = T + P
    IDLE = E * REGION
    GROUP = J // B
    SUMS = 2
    FIRST = E // 2
    ACT_PADS = J
    TABLE_TURN = 8
    UNITS = J * SH

    with ExitStack() as stack:
        def sb(name, shape, dt=F32):
            return stack.enter_context(nc.sbuf_tensor(name, shape, dt))

        def bank(name):
            return stack.enter_context(nc.psum_tensor(name, [P, 512], F32))

        def sem(name):
            return stack.enter_context(nc.semaphore(name))

        rows_dram = nc.dram_tensor("rows_dram", [IDLE + P, ROW], F32, kind="Internal").ap()
        sums_dram = [nc.dram_tensor(f"sum{i}_dram", [T + P, H], F32, kind="Internal").ap() for i in range(SUMS)]

        wgu = sb("wgu", [P, E, K, 2 * M])
        wd0 = sb("wd0", [P, E, H])
        wd1 = sb("wd1", [M2, E, H])
        sgu = sb("sgu", [P, SH, K, 2 * M])
        sd0 = sb("sd0", [P, SH, H])
        sd1 = sb("sd1", [M2, SH, H])
        xs = sb("xs", [P, J, H])
        rows = sb("rows", [P, J, ROW])
        xn = rows[:, :, 0:H]
        comb = rows[:, :, H:H + E]
        xnT = sb("xnT", [P, K, T])
        ctxT = xnT[0:D, 0, :]
        ident = sb("ident", [P, P])
        before = sb("before", [P, P], BF16)
        ones = sb("ones", [P, P], BF16)
        pad_rows = sb("pad_rows", [P, ROW])
        region = sb("region", [P, E])
        region_i = sb("region_i", [P, E], I32)
        part_i = sb("part_i", [P, 1], I32)
        part_f = sb("part_f", [P, 1])
        wij = sb("wij", [D, 2])
        wj_wide = sb("wj_wide", [D, P])
        badj = sb("badj", [P, 1])
        gates = sb("gates", [P, 2])
        tg = sb("tg", [P, 2])
        kx = sb("kx", [P, 2])
        cb = sb("cb", [P, E])
        wr = sb("wr", [P, K, E])
        stats = sb("stats", [P, J, 6])
        mv = sb("mv", [P, J, 2])
        rstd = sb("rstd", [P, J])
        rstd2 = sb("rstd2", [P, J])
        power = sb("power", [P, J])
        xa = sb("xa", [P, J])
        xc = sb("xc", [P, J])
        sib = sb("sib", [P, J])
        scores = sb("scores", [P, J, E])
        gkey = sb("gkey", [P, J, GROUPS + 8 - TOPK_GROUPS])
        gmark = sb("gmark", [P, J, GROUPS + 8 - TOPK_GROUPS])
        best = sb("best", [P, J, 8])
        key = sb("key", [P, J, E + 8 - TOPK])
        mark = sb("mark", [P, J, E + 8 - TOPK])
        chosen = sb("chosen", [P, J, E])
        chosen_b = sb("chosen_b", [P, J, E], BF16)
        cnt_i = sb("cnt_i", [P, 2, E], I32)
        ntile = sb("ntile", [P, E])
        tend = sb("tend", [P, E])
        tbase = sb("tbase", [P, E])
        zero_e = sb("zero_e", [P, E])
        row_i = sb("row_i", [P, J, 8], I32)
        past = sb("past", [P, E])
        cur = sb("cur", [P, E])
        tile_of = sb("tile_of", [P, 2])
        used = sb("used", [P, 1])
        tiles = sb("tiles", [2, P], I32)
        pad_at = sb("pad_at", [1, E], I32)
        idx = sb("idx", [P, RING], I32)
        wt = sb("wt", [P, RING])
        sg = sb("sg", [P, 2, M])
        h = sb("h", [P, 2, M])
        hT = sb("hT", [P, 2, 2, P])
        work = sb("work", [P, 4, H])
        rows_flat = rows[:, :, :].rearrange("p j c -> p (j c)")
        xg = rows_flat[:, 0:RING * ROW].rearrange("p (s c) -> p s c", s=RING)
        xT = rows_flat[:, RING * ROW:RING * ROW + 2 * H].rearrange("p (s k t) -> p s k t", s=2, k=K)
        sums = [w.rearrange("p (j c) -> p j c", c=H) for w in
                (rows_flat[:, 0:J * H], xnT[:, :, :].rearrange("p k t -> p (k t)"))]
        LAST_SUM = (TILES - 1) % SUMS
        ends = [(1 - LAST_SUM, sums[0]), (LAST_SUM, sums[1])]
        ctx_sb = work[:, 0:2, :].rearrange("p a (b d) -> p (a b) d", d=D)
        sig = work[:, 0:4, :]
        sfc = work[:, 0, :].rearrange("p (j e) -> p j e", e=E)
        y = xnT[:, :, :].rearrange("p k t -> p (k t)")[:, 0:RING * H].rearrange("p (s c) -> p s c", s=RING)
        scoresT = hT[0:E, :, :, :].rearrange("p a k t -> p (a k t)")[:, 0:GROUP * P]
        pair = chosen[:, :, :].rearrange("p j e -> p (j e)").rearrange("p (a b) -> p a b", a=4)

        pX = [bank(f"pX{i}") for i in range(2)]
        pG = [bank(f"pG{i}") for i in range(2)]
        pH = [bank(f"pH{i}") for i in range(2)]
        pY = [bank(f"pY{i}") for i in range(2)]
        sj_banks = [pG[0], pG[1], pY[0], pY[1]]
        xn_banks = [pX[0], pX[1], pG[0], pG[1]]
        si_bank, logit_bank, score_bank = pH[0], pH[0], pH[1]
        pos_banks = [pX[0], pX[1], pX[0], pX[1]]
        count_bank, table_bank = pX[0], pX[1]

        s_xin = [sem(f"s_xin{b}") for b in range(B)]
        s_ctx, s_small, s_cb, s_wr = sem("s_ctx"), sem("s_small"), sem("s_cb"), sem("s_wr")
        s_shw, s_expw = sem("s_shw"), [sem("s_expw0"), sem("s_expw1")]
        s_const, s_clear = sem("s_const"), sem("s_clear")
        s_dve = sem("s_dve")
        s_pool = sem("s_pool")
        s_table = sem("s_table")
        s_tanh, s_ctxT, s_ctxTc, s_wide, s_sj, s_sib = (sem(n) for n in
            ("s_tanh", "s_ctxT", "s_ctxTc", "s_wide", "s_sj", "s_sib"))
        s_var, s_rstd, s_sig, s_x1 = sem("s_var"), sem("s_rstd"), sem("s_sig"), sem("s_x1")
        s_xn, s_xnT, s_xnTc, s_logit, s_scoreT, s_scored, s_score = (sem(n) for n in
            ("s_xn", "s_xnT", "s_xnTc", "s_logit", "s_scoreT", "s_scored", "s_score"))
        s_chosen, s_pos, s_count, s_slot, s_tile_of, s_tableT, s_tiles, s_pad_at = (sem(n) for n in
            ("s_chosen", "s_pos", "s_count", "s_slot", "s_tile_of", "s_tableT", "s_tiles", "s_pad_at"))
        s_pads, s_scat = sem("s_pads"), sem("s_scat")
        s_gu, s_silu, s_h, s_hT, s_hTc, s_y, s_yc = (sem(n) for n in
            ("s_gu", "s_silu", "s_h", "s_hT", "s_hTc", "s_y", "s_yc"))
        s_xT, s_xTc, s_taken = sem("s_xT"), sem("s_xTc"), sem("s_taken")
        s_go = sem("s_go")
        s_load = [sem(f"s_load{i}") for i in range(RING)]
        s_add = [sem(f"s_add{i}") for i in range(RING)]
        s_sums = [[sem(f"s_sum{i}_{b}") for b in range(B)] for i in range(SUMS)]
        s_fin, s_out = sem("s_fin"), sem("s_out")

        x_rows = x.rearrange("b (h p) c -> p (b h) c", p=P)
        out_rows = out.rearrange("b (h p) c -> p (b h) c", p=P)
        block = stack.enter_context(nc.Block())

        def load_experts(eng, half):
            for e in range(half * FIRST, (half + 1) * FIRST, 4):
                for w, cols in ((gate_w, slice(0, M)), (up_w, slice(M, 2 * M))):
                    eng.dma_start(wgu[:, e:e + 4, :, cols].rearrange("p e k m -> p (e k) m"),
                                  w[e:e + 4].rearrange("e (k p) m -> p (e k) m", p=P)).then_inc(s_expw[half], 16)
                eng.dma_start(wd0[:, e:e + 4, :], down_w[e:e + 4, 0:P, :].rearrange("e p c -> p e c")).then_inc(s_expw[half], 16)
                eng.dma_start(wd1[:, e:e + 4, :], down_w[e:e + 4, P:M, :].rearrange("e p c -> p e c")).then_inc(s_expw[half], 16)

        @block.sync
        def _(sp):
            sp.dma_start(ctx_sb, ctx.rearrange("b (h p) d -> p (b h) d", p=P)).then_inc(s_ctx, 16)
            for b in range(B):
                sp.dma_start(xs[:, b * HALVES:(b + 1) * HALVES, :],
                             x_rows[:, b * HALVES:(b + 1) * HALVES, :]).then_inc(s_xin[b], 16)
            sp.dma_start(wr[:, :, :], w_router.rearrange("(k p) e -> p k e", p=P)).then_inc(s_wr, 16)
            for s in range(SH):
                cols = slice(s * M, (s + 1) * M)
                sp.dma_start(sgu[:, s, :, 0:M], sh_gate_w[:, cols].rearrange("(k p) m -> p k m", p=P)).then_inc(s_shw, 16)
                sp.dma_start(sgu[:, s, :, M:2 * M], sh_up_w[:, cols].rearrange("(k p) m -> p k m", p=P)).then_inc(s_shw, 16)
                sp.dma_start(sd0[:, s, :], sh_down_w[s * M:s * M + P, :]).then_inc(s_shw, 16)
                sp.dma_start(sd1[:, s, :], sh_down_w[s * M + P:(s + 1) * M, :]).then_inc(s_shw, 16)
            load_experts(sp, 0)
            load_experts(sp, 1)
            sp.wait_ge(s_const, 4)
            sp.dma_start(rows_dram[IDLE:IDLE + P, :], pad_rows[:, :]).then_inc(s_pads, 16)
            sp.wait_ge(s_pad_at, 1)
            with sp.Fori(0, (E - ACT_PADS) // 4) as q:
                for i in range(4):
                    at = sp.value_load(pad_at[0:1, bass.ds(q * 4 + i, 1)], min_val=0, max_val=IDLE - P)
                    sp.dma_start(rows_dram[bass.ds(at, P), :], pad_rows[:, :]).then_inc(s_pads, 16)
            sp.wait_ge(s_pads, 16 * (E + 1))
            sp.wait_ge(s_scat, 16 * J * TOPK)
            sp.wait_ge(s_tiles, 1)

            def load(t, s):
                at = sp.value_load(tiles[1:2, bass.ds(t, 1)], min_val=0, max_val=IDLE)
                sp.dma_start(xg[:, s, :], rows_dram[bass.ds(at, P), :]).then_inc(s_load[s], 16)

            def reload(i, s):
                t = i * RING + s
                sp.wait_ge(s_xT, t - (RING - 1))
                sp.wait_ge(s_taken, t - (RING - 1))
                load(t, s)

            for s in range(RING):
                load(s, s)
            with sp.Fori(1, FULL) as i:
                for s in range(RING):
                    reload(i, s)
            for s in range(REST):
                reload(FULL, s)
            sp.wait_ge(s_taken, TILES)
            sp.wait_ge(s_xTc, TILES)
            for i, into in ends:
                for s in range(i, RING, SUMS):
                    sp.wait_ge(s_add[s], 16 * (FULL + (s < REST)))
                for b in range(B):
                    js = slice(b * HALVES, (b + 1) * HALVES)
                    sp.dma_start(into[:, js, :],
                                 sums_dram[i][0:T, :].rearrange("(j p) c -> p j c", p=P)[:, js, :]).then_inc(s_sums[i][b], 16)
            for b in range(B):
                sp.wait_ge(s_fin, b + 1)
                sp.dma_start(out_rows[:, b * HALVES:(b + 1) * HALVES, :],
                             xs[:, b * HALVES:(b + 1) * HALVES, :]).then_inc(s_out, 16)
            sp.wait_ge(s_out, 16 * B)

        @block.gpsimd
        def _(pool):
            made = [0]

            def chain(ins):
                made[0] += 1
                ins.then_inc(s_pool, 1)
                pool.wait_ge(s_pool, made[0])

            chain(pool.memset(ident[:, :], 0.0))
            pool.affine_select(out=ident[:, :], in_=ident[:, :], compare_op=ALU.not_equal, fill=1.0,
                               base=0, pattern=[[-1, P]], channel_multiplier=1).then_inc(s_const, 1)
            pool.memset(power[:, :], -0.5)
            pool.memset(ones[:, :], 1.0).then_inc(s_const, 1)
            chain(pool.memset(before[:, :], 0.0))
            chain(pool.affine_select(out=before[:, :], in_=before[:, :], compare_op=ALU.is_ge, fill=1.0,
                                     base=0, pattern=[[-1, P]], channel_multiplier=1))
            pool.iota(part_i[:, :], pattern=[[0, 1]], base=0, channel_multiplier=1)
            chain(pool.iota(region_i[:, :], pattern=[[REGION, E]], base=1, channel_multiplier=0))
            pool.tensor_copy(region[:, :], region_i[:, :])
            pool.tensor_copy(part_f[:, :], part_i[:, :])
            pool.iota(rows[:, :, H + E:ROW].bitcast(I32).rearrange("p j o -> p (j o)"), pattern=[[P, J]], base=0,
                      channel_multiplier=1).then_inc(s_const, 1)
            chain(pool.memset(pad_rows[:, :], 0.0))
            chain(pool.iota(pad_rows[:, H + E:ROW].bitcast(I32), pattern=[[0, 1]], base=T, channel_multiplier=1))
            pool.sem_inc(s_const, 1)
            pool.wait_ge(s_var, 1)
            pool.tensor_tensor(out=rstd[:, :], in0=rstd[:, :], in1=power[:, :], op=ALU.pow).then_inc(s_rstd, 1)
            for b in range(B):
                g = slice(b * GROUP, (b + 1) * GROUP)
                pool.wait_ge(s_var, b + 2)
                pool.tensor_tensor(out=rstd2[:, g], in0=rstd2[:, g], in1=power[:, g], op=ALU.pow).then_inc(s_rstd, 1)
            for i in range(SUMS):
                pool.dma_start(sums_dram[i].rearrange("(j p) c -> p j c", p=P),
                               pad_rows[:, 0:H].unsqueeze(1).to_broadcast([P, J + 1, H])).then_inc(s_clear, 16)
            for j in range(J):
                pool.wait_ge(s_slot, j // GROUP + 1)
                for k in range(TOPK):
                    pool.indirect_dma_start(rows_dram[:, :], bass.IndirectOffsetOnAxis(ap=row_i[:, j, k:k + 1], axis=0),
                                            rows[:, j, :], None).then_inc(s_scat, 16)
            pool.wait_ge(s_clear, 16 * SUMS)

            def turn(i, s, first=False):
                t = i * RING + s
                if not first or s >= SUMS:
                    pool.wait_ge(s_add[(s - SUMS) % RING], 16 * i + (16 if s >= SUMS else 0))
                pool.wait_ge(s_yc, t + (J + 1))
                pool.sem_inc(s_go, 1)
                pool.indirect_dma_start(sums_dram[s % SUMS][:, :], bass.IndirectOffsetOnAxis(ap=idx[:, s:s + 1], axis=0),
                                        y[:, s, :], None, compute_op=ALU.add).then_inc(s_add[s], 16)

            for s in range(RING):
                turn(0, s, first=True)
            with pool.Fori(1, FULL) as i:
                for s in range(RING):
                    turn(i, s)
            for s in range(REST):
                turn(FULL, s)

        @block.scalar
        def _(act):
            for c in range(2):
                act.dma_start(wij[:, c:c + 1], w_adj[:, c * D:(c + 1) * D].rearrange("o d -> d o")).then_inc(s_small, 16)
            act.dma_start(gates[:, 0:1], g_xattn.partition_broadcast(P)).then_inc(s_small, 16)
            act.dma_start(gates[:, 1:2], g_ffn.partition_broadcast(P)).then_inc(s_small, 16)
            act.dma_start(badj[:, :], b_adj.partition_broadcast(P)).then_inc(s_small, 16)
            act.dma_start(cb[:, :], corr_bias.partition_broadcast(P)).then_inc(s_cb, 16)
            act.wait_ge(s_small, 80)
            nc.scalar.activation(tg[:, :], gates[:, :], ACT.Sigmoid).then_inc(s_table, 1)
            act.wait_ge(s_table, 1)
            nc.scalar.activation(tg[:, :], gates[:, :], ACT.Tanh).then_inc(s_tanh, 1)
            for c in range(2):
                act.wait_ge(s_ctxT, c + 1)
                nc.scalar.activation(ctxT[:, c * 512:(c + 1) * 512], pX[c][0:D, :], ACT.Copy).then_inc(s_ctxTc, 1)
            act.wait_ge(s_sib, 1)
            for j in range(J):
                nc.scalar.activation(xs[:, j, :], xs[:, j, :], ACT.Identity, scale=xa[:, j:j + 1],
                                     bias=xc[:, j:j + 1]).then_inc(s_sig, 1)
                if j % HALVES == 0:
                    act.wait_ge(s_sj, j // HALVES + 2)
                if j >= 4:
                    act.wait_ge(s_x1, j - 3)
                nc.scalar.activation(sig[:, j % 4, :], sj_banks[j // HALVES][:, 0:N], ACT.Sigmoid,
                                     bias=sib[:, j:j + 1]).then_inc(s_sig, 1)
            for b in range(B):
                for j in range(b * GROUP, (b + 1) * GROUP):
                    act.wait_ge(s_xnT, j + 1)
                    nc.scalar.activation(xnT[:, :, j * P:(j + 1) * P],
                                         xn_banks[j % 4][:, 0:K * P].rearrange("p (k t) -> p k t", k=K),
                                         ACT.Copy).then_inc(s_xnTc, 1)
                act.wait_ge(s_logit, b + 1)
                nc.scalar.activation(scoresT[:, :], logit_bank[0:E, 0:GROUP * P], ACT.Sigmoid).then_inc(s_scoreT, 1)
                act.wait_ge(s_scored, b + 1)
                nc.scalar.activation(scores[:, b * GROUP:(b + 1) * GROUP, :].rearrange("p j e -> p (j e)"),
                                     score_bank[:, 0:GROUP * E], ACT.Copy).then_inc(s_score, 1)

            def silu(n, par):
                act.wait_ge(s_gu, n + 1)
                nc.scalar.activation(sg[:, par, :], pG[par][:, 0:M], ACT.Silu).then_inc(s_silu, 1)

            for n in range(UNITS):
                silu(n, n % 2)
                if n >= UNITS - ACT_PADS:
                    e = E - UNITS + n
                    act.wait_ge(s_pad_at, 1)
                    at = act.value_load(pad_at[0:1, e:e + 1], min_val=0, max_val=IDLE - P)
                    act.dma_start(rows_dram[bass.ds(at, P), :], pad_rows[:, :]).then_inc(s_pads, 16)

            def copy_xT(t, par):
                act.wait_ge(s_xT, t + 1)
                nc.scalar.activation(xT[:, par, :, :].rearrange("p k t -> p (k t)"), pX[par][:, 0:K * P],
                                     ACT.Copy).then_inc(s_xTc, 1)

            def scale_y(t, s, reused, i):
                act.wait_ge(s_y, t + (J + 1))
                act.wait_ge(s_taken, t + 1)
                if reused:
                    act.wait_ge(s_add[s], i * 16)
                nc.scalar.activation(y[:, s, :], pY[s % 2][:, 0:H], ACT.Copy, scale=wt[:, s:s + 1]).then_inc(s_yc, 1)

            copy_xT(0, 0)
            copy_xT(1, 1)
            silu(UNITS, 0)

            def turn(i, s, left=RING, rounds=2):
                t = i * RING + s
                if left > 2:
                    copy_xT(t + 2, s % 2)
                if left > 1:
                    silu(t + (UNITS + 1), (s + 1) % 2)
                if s:
                    scale_y(t - 1, s - 1, rounds > 0, i)
                elif rounds:
                    scale_y(t - 1, RING - 1, rounds > 1, i - 1)

            for i in range(2):
                for s in range(RING):
                    turn(i, s, rounds=i)
            with act.Fori(2, FULL - 1) as i:
                for s in range(RING):
                    turn(i, s)
            for t in range((FULL - 1) * RING, TILES):
                turn(t // RING, t % RING, TILES - t)
            scale_y(TILES - 1, (TILES - 1) % RING, True, (TILES - 1) // RING)

        @block.tensor
        def _(pe):
            pe.wait_ge(s_const, 1)
            pe.wait_ge(s_ctx, 16)
            for j in range(J):
                ins = nc.tensor.transpose(pX[j // 4][0:D, (j % 4) * P:(j % 4 + 1) * P], ctx_sb[:, j, :], ident[:, :])
                if j % 4 == 3:
                    ins.then_inc(s_ctxT, 1)
            pe.wait_ge(s_small, 80)
            pe.wait_ge(s_wide, 1)
            pe.wait_ge(s_ctxTc, 2)
            for j in range(J):
                ins = nc.tensor.matmul(si_bank[:, j:j + 1], ctxT[:, j * P:(j + 1) * P], wij[:, 0:1], start=True, stop=True)
            ins.then_inc(s_sj, 1)
            for b in range(B):
                nc.tensor.matmul(sj_banks[b][:, 0:N], wj_wide[:, :],
                                 ctxT[:, b * N:(b + 1) * N], start=True, stop=True).then_inc(s_sj, 1)

            def router(b):
                for j in range(b * GROUP, (b + 1) * GROUP):
                    pe.wait_ge(s_xn, j + 1)
                    if j >= 4:
                        pe.wait_ge(s_xnTc, j - 3)
                    for k in range(K):
                        ins = nc.tensor.transpose(xn_banks[j % 4][:, k * P:(k + 1) * P], xn[:, j, k * P:(k + 1) * P], ident[:, :])
                    ins.then_inc(s_xnT, 1)
                pe.wait_ge(s_xnTc, (b + 1) * GROUP)
                for k in range(K):
                    ins = nc.tensor.matmul(logit_bank[0:E, 0:GROUP * P], wr[:, k, :],
                                           xnT[:, k, b * GROUP * P:(b + 1) * GROUP * P], start=(k == 0), stop=(k == K - 1))
                ins.then_inc(s_logit, 1)
                pe.wait_ge(s_scoreT, b + 1)
                if b:
                    pe.wait_ge(s_score, b)
                for g in range(GROUP):
                    ins = nc.tensor.transpose(score_bank[:, g * E:(g + 1) * E], scoresT[:, g * P:(g + 1) * P], ident[0:E, 0:E])
                ins.then_inc(s_scored, 1)

            def places(b):
                pe.wait_ge(s_chosen, b + 1)
                if b >= 2:
                    pe.wait_ge(s_slot, b - 1)
                mine = chosen_b[:, b * GROUP:(b + 1) * GROUP, :]
                place = pos_banks[b][:, 0:GROUP * E]
                nc.tensor.matmul(place, before[:, :], mine.rearrange("p j e -> p (j e)"), start=True, stop=False)
                for j in range(b * GROUP):
                    nc.tensor.matmul(place.rearrange("p (j e) -> p j e", e=E), ones[:, :],
                                     chosen_b[:, j:j + 1, :].to_broadcast([P, GROUP, E]), start=False, stop=False)
                for d in range(1, GROUP):
                    ins = nc.tensor.matmul(pos_banks[b][:, d * E:GROUP * E], ones[:, :],
                                           mine[:, 0:GROUP - d, :].rearrange("p j e -> p (j e)"),
                                           start=False, stop=(d == GROUP - 1))
                ins.then_inc(s_pos, 1)

            def gate_up(n, par, left, w):
                for k in range(K):
                    ins = nc.tensor.matmul(pG[par][:, 0:2 * M], left(k), w(k), start=(k == 0), stop=(k == K - 1))
                ins.then_inc(s_gu, 1)

            def turn_h(n, par):
                pe.wait_ge(s_h, n + 1)
                nc.tensor.transpose(pH[par][:, 0:P], h[:, par, 0:P], ident[:, :])
                nc.tensor.transpose(pH[par][0:M2, P:2 * P], h[:, par, P:M], ident[:, :]).then_inc(s_hT, 1)

            def down(n, par, bank, w0, w1, start, stop):
                nc.tensor.matmul(bank[:, 0:H], hT[:, par, 0, :], w0, start=start, stop=False)
                ins = nc.tensor.matmul(bank[:, 0:H], hT[0:M2, par, 1, :], w1, start=False, stop=stop)
                if stop:
                    ins.then_inc(s_y, 1)

            def shared_gate_up(n):
                gate_up(n, n % 2, lambda k: xnT[:, k, (n // SH) * P:(n // SH + 1) * P], lambda k: sgu[:, n % SH, k, :])

            def shared_down(n):
                j, part = n // SH, n % SH
                if part == 0 and j >= 2:
                    pe.wait_ge(s_yc, j - 1)
                down(n, n % 2, pY[j % 2], sd0[:, part, :], sd1[:, part, :], part == 0, part == SH - 1)

            def shared_turn(n):
                if n + 1 < UNITS:
                    shared_gate_up(n + 1)
                turn_h(n, n % 2)
                if n:
                    shared_down(n - 1)

            pe.wait_ge(s_wr, 16)
            for b in range(B - 1):
                router(b)
            pe.wait_ge(s_const, 3)
            places(0)
            router(B - 1)
            pe.wait_ge(s_shw, 16 * 4 * SH)
            shared_gate_up(0)
            for b in range(1, B):
                shared_turn(b - 1)
                places(b)
            pe.wait_ge(s_slot, B - 1)
            for j in range(J):
                ins = nc.tensor.matmul(count_bank[:, 0:E], ones[:, :], chosen_b[:, j, :], start=(j == 0), stop=(j == J - 1))
            ins.then_inc(s_count, 1)
            for n in range(B - 1, TABLE_TURN):
                shared_turn(n)
            pe.wait_ge(s_tile_of, 1)
            nc.tensor.transpose(table_bank[0:2, 0:P], tile_of[:, :], ident[:, :]).then_inc(s_tableT, 1)
            for n in range(TABLE_TURN, UNITS):
                shared_turn(n)
            pe.wait_ge(s_hTc, UNITS)
            shared_down(UNITS - 1)
            pe.wait_ge(s_tiles, 1)

            def transpose_x(s, rounds, par):
                pe.wait_ge(s_load[s], 16 * rounds)
                for k in range(K):
                    ins = nc.tensor.transpose(pX[par][:, k * P:(k + 1) * P], xg[:, s, k * P:(k + 1) * P], ident[:, :])
                ins.then_inc(s_xT, 1)

            def routed_gate_up(t, par, e):
                pe.wait_ge(s_xTc, t + 1)
                gate_up(None, par, lambda k: xT[:, par, k, :], lambda k: wgu[:, bass.ds(e, 1), k, :])

            pe.wait_ge(s_expw[0], 16 * FIRST)

            def look_up(t):
                return pe.value_load(tiles[0:1, bass.ds(t, 1)], min_val=0, max_val=E - 1)

            transpose_x(0, 1, 0)
            transpose_x(1, 1, 1)
            e_first = look_up(0)
            routed_gate_up(0, 0, e_first)

            def routed_down(t, par, e):
                down(t + UNITS, par, pY[par], wd0[:, bass.ds(e, 1), :], wd1[:, bass.ds(e, 1), :], True, True)

            def iteration(i, first=False, tiles=None):
                before_e = None if first else look_up(i * RING - 1)
                e = look_up(i * RING)
                for s in range(tiles or RING):
                    left = tiles - s if tiles else RING
                    t = i * RING + s
                    e_next = None
                    if left > 2:
                        transpose_x((s + 2) % RING, i + (s + 2) // RING + 1, s % 2)
                    if left > 1:
                        e_next = look_up(t + 1)
                        routed_gate_up(t + 1, (s + 1) % 2, e_next)
                    turn_h(t + UNITS, s % 2)
                    if before_e is not None:
                        routed_down(t - 1, (s + 1) % 2, before_e)
                    before_e, e = e, e_next
                return before_e

            early = (FIRST - 1) // RING
            iteration(0, first=True)
            with pe.Fori(1, early) as i:
                iteration(i)
            pe.wait_ge(s_expw[1], 16 * FIRST)
            with pe.Fori(early, FULL - 1) as i:
                iteration(i)
            e_last = iteration(FULL - 1, tiles=RING + REST)
            pe.wait_ge(s_hTc, TILES + UNITS)
            pe.wait_ge(s_yc, TILES - 2 + J)
            routed_down(TILES - 1, (TILES - 1) % 2, e_last)

        @block.vector
        def _(dve):
            made = [0]
            V = nc.vector

            def link(ins):
                made[0] += 1
                ins.then_inc(s_dve, 1)
                dve.wait_ge(s_dve, made[0])

            dve.wait_ge(s_small, 80)
            V.tensor_copy(wj_wide[:, :], wij[:, 1:2].to_broadcast([D, P])).then_inc(s_wide, 1)
            V.memset(gkey[:, :, :], ABSENT)
            V.memset(key[:, :, :], ABSENT)
            V.memset(zero_e[:, :], 0.0)

            for j in range(J):
                if j % HALVES == 0:
                    dve.wait_ge(s_xin[j // HALVES], 16)
                ins = V.bn_stats(stats[:, j, :], xs[:, j, :])
            link(ins)
            for j in range(J):
                ins = V.bn_aggr(mv[:, j, :], stats[:, j, :])
            link(ins)
            V.tensor_scalar(rstd[:, :], mv[:, :, 1], EPS, None, ALU.add).then_inc(s_var, 1)
            dve.wait_ge(s_tanh, 1)
            V.tensor_scalar(kx[:, 0:1], tg[:, 0:1], 1.0 - P_ASEM, None, ALU.mult)
            link(V.tensor_scalar(kx[:, 1:2], tg[:, 0:1], P_ASEM, None, ALU.mult))
            dve.wait_ge(s_rstd, 1)
            link(V.tensor_scalar(xa[:, :], rstd[:, :], kx[:, 0:1], None, ALU.mult))
            link(V.scalar_tensor_tensor(xc[:, :], mv[:, :, 0], -1.0, xa[:, :], op0=ALU.mult, op1=ALU.mult))
            link(V.tensor_scalar(xa[:, :], xa[:, :], 1.0, None, ALU.add))
            dve.wait_ge(s_sj, 1)
            V.tensor_scalar(sib[:, :], si_bank[:, 0:J], badj[:, 0:1], None, ALU.add).then_inc(s_sib, 1)

            def norm_group(b):
                dve.wait_ge(s_rstd, b + 2)
                for j in range(b * GROUP, (b + 1) * GROUP):
                    V.tensor_scalar(xn[:, j, :], xs[:, j, :], mv[:, j, 0:1], rstd2[:, j:j + 1],
                                    ALU.subtract, ALU.mult).then_inc(s_xn, 1)

            for b in range(B):
                js = range(b * GROUP, (b + 1) * GROUP)
                for j in js:
                    dve.wait_ge(s_sig, 2 * j + 2)
                    ins = V.scalar_tensor_tensor(xs[:, j, :], sig[:, j % 4, :], kx[:, 1:2], xs[:, j, :],
                                                 op0=ALU.mult, op1=ALU.add).then_inc(s_x1, 1)
                dve.wait_ge(s_x1, js.stop)
                for j in js:
                    ins = V.bn_stats(stats[:, j, :], xs[:, j, :])
                link(ins)
                for j in js:
                    ins = V.bn_aggr(mv[:, j, :], stats[:, j, :])
                link(ins)
                V.tensor_scalar(rstd2[:, js.start:js.stop], mv[:, js.start:js.stop, 1], EPS, None, ALU.add).then_inc(s_var, 1)
                if b:
                    norm_group(b - 1)
            norm_group(B - 1)

            dve.wait_ge(s_cb, 16)
            dve.wait_ge(s_const, 4)

            def choose(js, marks, keys, n, top):
                for j in js:
                    ins = V.max(best[:, j, :], keys[:, j, 0:n])
                link(ins)
                link(V.memset(best[:, js.start:js.stop, top:8], ABSENT))
                for j in js:
                    ins = V.match_replace(out=marks[:, j, :], in_to_replace=best[:, j, :], in_values=keys[:, j, :],
                                          imm_value=CHOSEN)
                link(ins)

            def choose_experts(b):
                js = range(b * GROUP, (b + 1) * GROUP)
                g = slice(js.start, js.stop)
                dve.wait_ge(s_score, b + 1)
                link(V.tensor_tensor(sfc[:, g, :], scores[:, g, :],
                                     cb[:, :].unsqueeze(1).to_broadcast([P, GROUP, E]), ALU.add))
                four = sfc[:, g, :].rearrange("p j (g e) -> p (j g) e", e=PER)
                a, c, d, f = (pair[:, i, g.start * GROUPS:g.stop * GROUPS] for i in range(4))
                V.tensor_tensor(a, four[:, :, 0], four[:, :, 1], ALU.max)
                V.tensor_tensor(c, four[:, :, 0], four[:, :, 1], ALU.min)
                V.tensor_tensor(d, four[:, :, 2], four[:, :, 3], ALU.max)
                link(V.tensor_tensor(f, four[:, :, 2], four[:, :, 3], ALU.min))
                link(V.tensor_tensor(c, c, f, ALU.max))
                link(V.tensor_tensor(f, a, d, ALU.min))
                V.tensor_tensor(a, a, d, ALU.max)
                link(V.tensor_tensor(c, c, f, ALU.max))
                link(V.tensor_tensor(gkey[:, g, 0:GROUPS], a.rearrange("p (j g) -> p j g", g=GROUPS),
                                     c.rearrange("p (j g) -> p j g", g=GROUPS), ALU.add))
                choose(js, gmark, gkey, GROUPS, TOPK_GROUPS)
                link(V.tensor_scalar(gmark[:, g, 0:GROUPS], gmark[:, g, 0:GROUPS], CHOSEN, BARRED, ALU.is_lt, ALU.mult))
                for j in js:
                    ins = V.tensor_tensor(key[:, j, 0:E].rearrange("p (g e) -> p g e", e=PER),
                                          sfc[:, j, :].rearrange("p (g e) -> p g e", e=PER),
                                          gmark[:, j, 0:GROUPS].unsqueeze(2).to_broadcast([P, GROUPS, PER]), ALU.add)
                link(ins)
                choose(js, mark, key, E, TOPK)
                V.tensor_scalar(chosen_b[:, g, :], mark[:, g, 0:E], CHOSEN, None, ALU.is_equal).then_inc(s_chosen, 1)
                link(V.tensor_scalar(chosen[:, g, :], mark[:, g, 0:E], CHOSEN, None, ALU.is_equal))
                V.scalar_tensor_tensor(comb[:, g, :], scores[:, g, :], tg[:, 1:2], chosen[:, g, :],
                                       op0=ALU.mult, op1=ALU.mult)

            def choose_rows(b):
                js = range(b * GROUP, (b + 1) * GROUP)
                g = slice(js.start, js.stop)
                dve.wait_ge(s_pos, b + 1)
                link(V.tensor_tensor(mark[:, g, 0:E], pos_banks[b][:, 0:GROUP * E].rearrange("p (j e) -> p j e", e=E),
                                     region[:, :].unsqueeze(1).to_broadcast([P, GROUP, E]), ALU.add))
                link(V.tensor_tensor(mark[:, g, 0:E], mark[:, g, 0:E], chosen[:, g, :], ALU.mult))
                for j in js:
                    ins = V.max(best[:, j, :], mark[:, j, 0:E])
                link(ins)
                V.tensor_scalar(row_i[:, g, :], best[:, g, :], -1.0, None, ALU.add).then_inc(s_slot, 1)

            def gate(n, par):
                dve.wait_ge(s_silu, n + 1)
                V.tensor_tensor(h[:, par, :], sg[:, par, :], pG[par][:, M:2 * M], ALU.mult).then_inc(s_h, 1)

            def copy_hT(n, par):
                dve.wait_ge(s_hT, n + 1)
                V.tensor_copy(hT[:, par, 0, :], pH[par][:, 0:P])
                V.tensor_copy(hT[0:M2, par, 1, :], pH[par][0:M2, P:2 * P]).then_inc(s_hTc, 1)

            def shared_out(j):
                dve.wait_ge(s_y, j + 1)
                V.scalar_tensor_tensor(xs[:, j, :], pY[j % 2][:, 0:H], tg[:, 1:2], xs[:, j, :],
                                       op0=ALU.mult, op1=ALU.add).then_inc(s_yc, 1)

            def shared_turn(n):
                copy_hT(n, n % 2)
                if n + 1 < UNITS:
                    gate(n + 1, (n + 1) % 2)
                if n >= SH + 1 and (n - 1) % SH == 0:
                    shared_out((n - 1) // SH - 1)

            choose_experts(0)
            choose_rows(0)
            gate(0, 0)
            for b in range(1, B):
                choose_experts(b)
                shared_turn(b - 1)
                choose_rows(b)

            dve.wait_ge(s_const, 4)
            dve.wait_ge(s_count, 1)
            link(V.tensor_copy(ntile[:, :], count_bank[:, 0:E]))
            V.scalar_tensor_tensor(pad_at[0:1, :], ntile[0:1, :], -1.0, region[0:1, :],
                                   op0=ALU.add, op1=ALU.add).then_inc(s_pad_at, 1)
            for n in range(B - 1, TABLE_TURN - 1):
                shared_turn(n)

            link(V.tensor_scalar(cnt_i[:, 0, :], ntile[:, :], float(P - 1), None, ALU.add))
            link(V.tensor_scalar(cnt_i[:, 1, :], cnt_i[:, 0, :], P.bit_length() - 1, None, ALU.logical_shift_right))
            link(V.tensor_scalar(ntile[:, :], cnt_i[:, 1, :], 1.0, None, ALU.max))
            link(V.tensor_tensor_scan(tend[:, :], ntile[:, :], zero_e[:, :], 0.0, ALU.add, ALU.add))
            link(V.tensor_tensor(tbase[:, :], tend[:, :], ntile[:, :], ALU.subtract))
            link(V.tensor_scalar(past[:, :], tend[:, :], part_f[:, 0:1], None, ALU.is_le))
            link(V.tensor_scalar(cur[:, :], tbase[:, :], part_f[:, 0:1], None, ALU.is_le))
            link(V.tensor_tensor(cur[:, :], cur[:, :], past[:, :], ALU.subtract))
            link(V.reduce_sum(used[:, :], cur[:, :], axis=mybir.AxisListType.X))
            link(V.reduce_sum(tile_of[:, 0:1], past[:, :], axis=mybir.AxisListType.X))
            link(V.tensor_scalar(tile_of[:, 0:1], tile_of[:, 0:1], float(E - 1), None, ALU.min))
            link(V.scalar_tensor_tensor(tbase[:, :], tbase[:, :], -float(P), region[:, :], op0=ALU.mult, op1=ALU.add))
            link(V.tensor_tensor(cur[:, :], cur[:, :], tbase[:, :], ALU.mult))
            link(V.reduce_sum(tile_of[:, 1:2], cur[:, :], axis=mybir.AxisListType.X))
            link(V.tensor_scalar(part_f[:, :], part_f[:, :], float(P), -float(IDLE + 1), ALU.mult, ALU.add))
            link(V.scalar_tensor_tensor(tile_of[:, 1:2], used[:, :], part_f[:, 0:1], tile_of[:, 1:2],
                                        op0=ALU.mult, op1=ALU.add))
            V.tensor_scalar(tile_of[:, 1:2], tile_of[:, 1:2], float(IDLE), None, ALU.add).then_inc(s_tile_of, 1)
            for n in range(TABLE_TURN - 1, TABLE_TURN + 1):
                shared_turn(n)
            dve.wait_ge(s_tableT, 1)
            V.tensor_copy(tiles[:, :], table_bank[0:2, 0:P]).then_inc(s_tiles, 1)
            dve.wait_ge(s_tiles, 1)
            for n in range(TABLE_TURN + 1, UNITS):
                shared_turn(n)
            shared_out(J - 1)

            def take(t, s, rounds, used=True):
                e = dve.value_load(tiles[0:1, bass.ds(t, 1)], min_val=0, max_val=E - 1)
                dve.wait_ge(s_load[s], 16 * rounds)
                V.tensor_copy(wt[:, s:s + 1], xg[:, s, bass.ds(e + H, 1)])
                if used:
                    dve.wait_ge(s_add[s], 16 * rounds - 16)
                V.tensor_copy(idx[:, s:s + 1], xg[:, s, H + E:ROW].bitcast(I32)).then_inc(s_taken, 1)

            take(0, 0, 1, used=False)
            gate(UNITS, 0)
            take(1, 1, 1, used=False)

            def turn(i, s, left=RING, first=False):
                t = i * RING + s
                copy_hT(t + UNITS, s % 2)
                if left > 1:
                    gate(t + (UNITS + 1), (s + 1) % 2)
                if left > 2:
                    take(t + 2, (s + 2) % RING, i + (s + 2) // RING + 1, used=not first or s + 2 >= RING)

            for s in range(RING):
                turn(0, s, first=True)
            with dve.Fori(1, FULL - 1) as i:
                for s in range(RING):
                    turn(i, s)
            for t in range((FULL - 1) * RING, TILES):
                turn(t // RING, t % RING, TILES - t)
            for i, routed in ends:
                for b in range(B):
                    js = slice(b * HALVES, (b + 1) * HALVES)
                    dve.wait_ge(s_sums[i][b], 16)
                    ins = V.tensor_tensor(xs[:, js, :], xs[:, js, :], routed[:, js, :], ALU.add)
                    if i == LAST_SUM:
                        ins.then_inc(s_fin, 1)
                if i != LAST_SUM:
                    link(ins)


_INS = ['x', 'ctx_512', 'g_xattn', 'g_ffn', 'L0_xattn_W', 'L0_xattn_b', 'L0_ffn_w_router', 'L0_ffn_corr_bias',
        'L0_ffn_gate_w', 'L0_ffn_up_w', 'L0_ffn_down_w', 'L0_ffn_sh_gate_w', 'L0_ffn_sh_up_w', 'L0_ffn_sh_down_w']
_OUTS = [((4, 256, 256), 'float32')]


def kernel(**inputs):
    import numpy as _np
    import concourse.bacc as _bacc
    from concourse import mybir as _mybir
    from concourse.bass_utils import run_bass_kernel_spmd as _run

    nc = _bacc.Bacc("TRN2", target_bir_lowering=False, num_devices=1)
    arrays, args = {}, []
    for name in _INS:
        a = _np.ascontiguousarray(inputs[name])
        arrays[f"in_{name}_dram"] = a
        args.append(nc.dram_tensor(f"in_{name}_dram", a.shape, _mybir.dt.from_np(a.dtype), kind="ExternalInput").ap())
    for i, (shape, dtype) in enumerate(_OUTS):
        dt = _mybir.dt.from_np(_np.dtype(dtype))
        args.append(nc.dram_tensor(f"out_{i}_dram", shape, dt, kind="ExternalOutput").ap())
    gated_xattn_moe(nc, *args)
    r = _run(nc, [arrays], core_ids=[0])
    got = tuple(r.results[0][f"out_{i}_dram"] for i in range(len(_OUTS)))
    return got[0]
```

```python
from contextlib import ExitStack

import concourse.bass as bass
from concourse import mybir

F32 = mybir.dt.float32
BF16 = mybir.dt.bfloat16
I32 = mybir.dt.int32
ALU = mybir.AluOpType
ACT = mybir.ActivationFunctionType

P = 128
P_ASEM = 0.6
EPS = 1e-5
TOPK = 6
GROUPS = 8
TOPK_GROUPS = 4
RING = 4
ABSENT = -3.0e38
CHOSEN = 3.0e38
BARRED = -1.0e30


def gated_xattn_moe(nc, x, ctx, g_xattn, g_ffn, w_adj, b_adj, w_router, corr_bias, gate_w, up_w, down_w,
                    sh_gate_w, sh_up_w, sh_down_w, out):
    B, N, H = x.shape
    D = ctx.shape[2]
    E, _, M = gate_w.shape
    T = B * N
    J = T // P
    HALVES = N // P
    K = H // P
    M2 = M - P
    SH = sh_gate_w.shape[1] // M
    PER = E // GROUPS
    PAIRS = T * TOPK
    TILES = (PAIRS - E) // P + E
    FULL, REST = TILES // RING, TILES % RING
    ROW = H + E + 1
    REGION = T + P
    IDLE = E * REGION
    GROUP = J // B
    PLACED = [range(0, GROUP), range(GROUP, 2 * GROUP), range(2 * GROUP, J)]
    SUMS = 2
    FIRST = E * 5 // 8
    LATE = 1 + (E - FIRST) // RING
    PAD_TURN = 7
    ACT_PADS = 12
    TABLE_TURN = 6
    UNITS = J * SH

    with ExitStack() as stack:
        def sb(name, shape, dt=F32):
            return stack.enter_context(nc.sbuf_tensor(name, shape, dt))

        def bank(name):
            return stack.enter_context(nc.psum_tensor(name, [P, 512], F32))

        def sem(name):
            return stack.enter_context(nc.semaphore(name))

        rows_dram = nc.dram_tensor("rows_dram", [IDLE + P, ROW], F32, kind="Internal").ap()
        sums_dram = [nc.dram_tensor(f"sum{i}_dram", [T + P, H], F32, kind="Internal").ap() for i in range(SUMS)]

        wgu = sb("wgu", [P, E, K, 2 * M])
        wd0 = sb("wd0", [P, E, H])
        wd1 = sb("wd1", [M2, E, H])
        sgu = sb("sgu", [P, SH, K, 2 * M])
        sd0 = sb("sd0", [P, SH, H])
        sd1 = sb("sd1", [M2, SH, H])
        xs = sb("xs", [P, J, H])
        rows = sb("rows", [P, J, ROW])
        xn = rows[:, :, 0:H]
        comb = rows[:, :, H:H + E]
        xnT = sb("xnT", [P, K, T])
        ctxT = xnT[0:D, 0, :]
        ident = sb("ident", [P, P])
        before = sb("before", [P, P], BF16)
        ones = sb("ones", [P, P], BF16)
        pad_rows = sb("pad_rows", [P, ROW])
        region = sb("region", [P, E])
        region_i = sb("region_i", [P, E], I32)
        part_i = sb("part_i", [P, 1], I32)
        part_f = sb("part_f", [P, 1])
        wij = sb("wij", [D, 2])
        wj_wide = sb("wj_wide", [D, P])
        badj = sb("badj", [P, 1])
        gates = sb("gates", [P, 2])
        tg = sb("tg", [P, 2])
        kx = sb("kx", [P, 2])
        cb = sb("cb", [P, E])
        wr = sb("wr", [P, K, E])
        stats = sb("stats", [P, J, 6])
        mv = sb("mv", [P, J, 2])
        rstd = sb("rstd", [P, J])
        rstd2 = sb("rstd2", [P, J])
        power = sb("power", [P, J])
        xa = sb("xa", [P, J])
        xc = sb("xc", [P, J])
        sib = sb("sib", [P, J])
        scores = sb("scores", [P, J, E])
        gkey = sb("gkey", [P, J, GROUPS + 8 - TOPK_GROUPS])
        gmark = sb("gmark", [P, J, GROUPS + 8 - TOPK_GROUPS])
        best = sb("best", [P, J, 8])
        key = sb("key", [P, J, E + 8 - TOPK])
        mark = sb("mark", [P, J, E + 8 - TOPK])
        chosen = sb("chosen", [P, J, E])
        chosen_b = sb("chosen_b", [P, J, E], BF16)
        cnt_i = sb("cnt_i", [P, 2, E], I32)
        ntile = sb("ntile", [P, E])
        tend = sb("tend", [P, E])
        tbase = sb("tbase", [P, E])
        zero_e = sb("zero_e", [P, E])
        row_i = sb("row_i", [P, J, 8], I32)
        past = sb("past", [P, E])
        cur = sb("cur", [P, E])
        tile_of = sb("tile_of", [P, 2])
        used = sb("used", [P, 1])
        tiles = sb("tiles", [2, P], I32)
        LEAST = -(-(E - REST) // RING) - 1
        round_ends = sb("round_ends", [1, FULL - 2])
        round_ends_i = sb("round_ends_i", [1, FULL - 2], I32)
        round_is = sb("round_is", [1, FULL - 2])
        last_f = sb("last_f", [1, 1])
        last_i = sb("last_i", [1, 1], I32)
        pad_at = sb("pad_at", [1, E], I32)
        idx = sb("idx", [P, RING], I32)
        wt = sb("wt", [P, RING])
        sg = sb("sg", [P, 2, M])
        h = sb("h", [P, 2, M])
        hT = sb("hT", [P, 2, 2, P])
        work = sb("work", [P, 4, H])
        rows_flat = rows[:, :, :].rearrange("p j c -> p (j c)")
        xg = rows_flat[:, 0:RING * ROW].rearrange("p (s c) -> p s c", s=RING)
        xT = rows_flat[:, RING * ROW:RING * ROW + 2 * H].rearrange("p (s k t) -> p s k t", s=2, k=K)
        sums = [w.rearrange("p (j c) -> p j c", c=H) for w in
                (rows_flat[:, 0:J * H], xnT[:, :, :].rearrange("p k t -> p (k t)"))]
        LAST_SUM = (TILES - 1) % SUMS
        ends = [(1 - LAST_SUM, sums[0]), (LAST_SUM, sums[1])]
        ctx_sb = work[:, 0:2, :].rearrange("p a (b d) -> p (a b) d", d=D)
        sig = work[:, 0:4, :]
        y = xnT[:, :, :].rearrange("p k t -> p (k t)")[:, 0:RING * H].rearrange("p (s c) -> p s c", s=RING)
        sfc = comb
        scoresT = hT[0:E, :, :, :].rearrange("p a k t -> p (a k t)")[:, 0:GROUP * P]
        pair = chosen[:, :, :].rearrange("p j e -> p (j e)").rearrange("p (a b) -> p a b", a=4)

        pX = [bank(f"pX{i}") for i in range(2)]
        pG = [bank(f"pG{i}") for i in range(2)]
        pH = [bank(f"pH{i}") for i in range(2)]
        pY = [bank(f"pY{i}") for i in range(2)]
        sj_banks = [pG[0], pG[1], pY[0], pY[1]]
        xn_banks = [pX[0], pX[1], pG[0], pG[1]]
        si_bank, logit_bank, score_bank = pH[0], pH[0], pH[1]
        pos_banks = [pY[0], pY[1], pX[1]]
        count_bank, table_bank = pX[0], pX[1]

        s_xin = [sem(f"s_xin{b}") for b in range(B)]
        s_ctx, s_wadj, s_gates, s_cb, s_wr = (sem(n) for n in ("s_ctx", "s_wadj", "s_gates", "s_cb", "s_wr"))
        s_shw, s_expw = sem("s_shw"), [sem("s_expw0"), sem("s_expw1")]
        s_const, s_clear = sem("s_const"), sem("s_clear")
        s_dve = sem("s_dve")
        s_pool = sem("s_pool")
        s_table = sem("s_table")
        s_tanh, s_ctxT, s_ctxTc, s_wide, s_sj, s_sib = (sem(n) for n in
            ("s_tanh", "s_ctxT", "s_ctxTc", "s_wide", "s_sj", "s_sib"))
        s_var, s_rstd, s_sig, s_x1 = sem("s_var"), sem("s_rstd"), sem("s_sig"), sem("s_x1")
        s_xn, s_xnT, s_xnTc, s_logit, s_scoreT, s_scored, s_score = (sem(n) for n in
            ("s_xn", "s_xnT", "s_xnTc", "s_logit", "s_scoreT", "s_scored", "s_score"))
        s_chosen, s_pos, s_count, s_slot, s_tile_of, s_tableT, s_tiles, s_pad_at = (sem(n) for n in
            ("s_chosen", "s_pos", "s_count", "s_slot", "s_tile_of", "s_tableT", "s_tiles", "s_pad_at"))
        s_pads, s_scat = sem("s_pads"), sem("s_scat")
        s_gu, s_silu, s_h, s_hT, s_hTc, s_y, s_yc = (sem(n) for n in
            ("s_gu", "s_silu", "s_h", "s_hT", "s_hTc", "s_y", "s_yc"))
        s_xT, s_xTc, s_taken = sem("s_xT"), sem("s_xTc"), sem("s_taken")
        s_go, s_passed = sem("s_go"), sem("s_passed")
        s_load = [sem(f"s_load{i}") for i in range(RING)]
        s_add = [sem(f"s_add{i}") for i in range(RING)]
        s_sums = [[sem(f"s_sum{i}_{b}") for b in range(B)] for i in range(SUMS)]
        s_fin, s_out = sem("s_fin"), sem("s_out")

        x_rows = x.rearrange("b (h p) c -> p (b h) c", p=P)
        out_rows = out.rearrange("b (h p) c -> p (b h) c", p=P)
        block = stack.enter_context(nc.Block())

        def load_last(eng):
            return eng.value_load(last_i[0:1, 0:1], min_val=LEAST - 1, max_val=FULL - 2) + 1

        def load_expert_weights(eng, n):
            e = n // 4 * 4
            if n % 4 < 2:
                w, cols = ((gate_w, slice(0, M)), (up_w, slice(M, 2 * M)))[n % 4]
                ins = eng.dma_start(wgu[:, e:e + 4, :, cols].rearrange("p e k m -> p (e k) m"),
                                    w[e:e + 4].rearrange("e (k p) m -> p (e k) m", p=P))
            elif n % 4 == 2:
                ins = eng.dma_start(wd0[:, e:e + 4, :], down_w[e:e + 4, 0:P, :].rearrange("e p c -> p e c"))
            else:
                ins = eng.dma_start(wd1[:, e:e + 4, :], down_w[e:e + 4, P:M, :].rearrange("e p c -> p e c"))
            ins.then_inc(s_expw[0 if e < FIRST else 1], 16)

        @block.sync
        def _(sp):
            sp.dma_start(ctx_sb, ctx.rearrange("b (h p) d -> p (b h) d", p=P)).then_inc(s_ctx, 16)
            for b in range(B):
                sp.dma_start(xs[:, b * HALVES:(b + 1) * HALVES, :],
                             x_rows[:, b * HALVES:(b + 1) * HALVES, :]).then_inc(s_xin[b], 16)
            sp.dma_start(gates[:, 0:1], g_xattn.partition_broadcast(P)).then_inc(s_gates, 16)
            sp.dma_start(gates[:, 1:2], g_ffn.partition_broadcast(P)).then_inc(s_gates, 16)
            sp.dma_start(badj[:, :], b_adj.partition_broadcast(P)).then_inc(s_gates, 16)
            sp.dma_start(cb[:, :], corr_bias.partition_broadcast(P)).then_inc(s_cb, 16)
            sp.dma_start(wr[:, :, :], w_router.rearrange("(k p) e -> p k e", p=P)).then_inc(s_wr, 16)
            for s in range(SH):
                cols = slice(s * M, (s + 1) * M)
                sp.dma_start(sgu[:, s, :, 0:M], sh_gate_w[:, cols].rearrange("(k p) m -> p k m", p=P)).then_inc(s_shw, 16)
                sp.dma_start(sgu[:, s, :, M:2 * M], sh_up_w[:, cols].rearrange("(k p) m -> p k m", p=P)).then_inc(s_shw, 16)
                sp.dma_start(sd0[:, s, :], sh_down_w[s * M:s * M + P, :]).then_inc(s_shw, 16)
                sp.dma_start(sd1[:, s, :], sh_down_w[s * M + P:(s + 1) * M, :]).then_inc(s_shw, 16)
            for n in range(FIRST):
                load_expert_weights(sp, n)
            sp.wait_ge(s_const, 4)
            sp.dma_start(rows_dram[IDLE:IDLE + P, :], pad_rows[:, :]).then_inc(s_pads, 16)
            sp.wait_ge(s_pad_at, 1)
            with sp.Fori(0, (E - ACT_PADS) // 4) as q:
                for i in range(4):
                    at = sp.value_load(pad_at[0:1, bass.ds(q * 4 + i, 1)], min_val=0, max_val=IDLE - P)
                    sp.dma_start(rows_dram[bass.ds(at, P), :], pad_rows[:, :]).then_inc(s_pads, 16)
            sp.wait_ge(s_tiles, 1)
            last = load_last(sp)

            def row_of(t):
                return sp.value_load(tiles[1:2, bass.ds(t, 1)], min_val=0, max_val=IDLE)

            first_row = row_of(0)
            sp.wait_ge(s_pads, 16 * (E + 1))
            sp.wait_ge(s_scat, 16 * J * TOPK)

            def load(t, s, at=None):
                at = row_of(t) if at is None else at
                sp.dma_start(xg[:, s, :], rows_dram[bass.ds(at, P), :]).then_inc(s_load[s], 16)

            def reload(i, s):
                t = i * RING + s
                sp.wait_ge(s_xT, t - (RING - 1))
                sp.wait_ge(s_taken, t - (RING - 1))
                load(t, s)

            load(0, 0, first_row)
            for s in range(1, RING):
                load(s, s)
            for i in range(1, LATE):
                for s in range(RING):
                    reload(i, s)
                    load_expert_weights(sp, FIRST + (i - 1) * RING + s)
            with sp.Fori(LATE, FULL) as i:
                with sp.If(i < last + 1):
                    for s in range(RING):
                        reload(i, s)
            for s in range(REST):
                reload(last + 1, s)
            sp.wait_ge(s_taken, last * RING + (RING + REST))
            sp.sem_inc(s_passed, 1)
            sp.wait_ge(s_xTc, last * RING + (RING + REST))
            sp.sem_inc(s_passed, 1)
            for i, into in ends:
                for s in range(i, RING, SUMS):
                    sp.wait_ge(s_add[s], (last + (2 if s < REST else 1)) * 16)
                    sp.sem_inc(s_passed, 1)
                for b in range(B):
                    js = slice(b * HALVES, (b + 1) * HALVES)
                    sp.dma_start(into[:, js, :],
                                 sums_dram[i][0:T, :].rearrange("(j p) c -> p j c", p=P)[:, js, :]).then_inc(s_sums[i][b], 16)
            for b in range(B):
                sp.wait_ge(s_fin, b + 1)
                sp.dma_start(out_rows[:, b * HALVES:(b + 1) * HALVES, :],
                             xs[:, b * HALVES:(b + 1) * HALVES, :]).then_inc(s_out, 16)
            sp.wait_ge(s_out, 16 * B)

        @block.gpsimd
        def _(pool):
            made = [0]

            def chain(ins):
                made[0] += 1
                ins.then_inc(s_pool, 1)
                pool.wait_ge(s_pool, made[0])

            chain(pool.memset(ident[:, :], 0.0))
            pool.affine_select(out=ident[:, :], in_=ident[:, :], compare_op=ALU.not_equal, fill=1.0,
                               base=0, pattern=[[-1, P]], channel_multiplier=1).then_inc(s_const, 1)
            pool.memset(power[:, :], -0.5)
            pool.memset(ones[:, :], 1.0).then_inc(s_const, 1)
            chain(pool.memset(before[:, :], 0.0))
            chain(pool.affine_select(out=before[:, :], in_=before[:, :], compare_op=ALU.is_ge, fill=1.0,
                                     base=0, pattern=[[-1, P]], channel_multiplier=1))
            pool.iota(part_i[:, :], pattern=[[0, 1]], base=0, channel_multiplier=1)
            chain(pool.iota(region_i[:, :], pattern=[[REGION, E]], base=1, channel_multiplier=0))
            chain(pool.iota(round_ends_i[:, :], pattern=[[RING, FULL - 2]], base=2 * RING + REST, channel_multiplier=0))
            pool.tensor_copy(round_ends[:, :], round_ends_i[:, :])
            pool.tensor_copy(region[:, :], region_i[:, :])
            pool.tensor_copy(part_f[:, :], part_i[:, :])
            pool.iota(rows[:, :, H + E:ROW].bitcast(I32).rearrange("p j o -> p (j o)"), pattern=[[P, J]], base=0,
                      channel_multiplier=1).then_inc(s_const, 1)
            chain(pool.memset(pad_rows[:, :], 0.0))
            chain(pool.iota(pad_rows[:, H + E:ROW].bitcast(I32), pattern=[[0, 1]], base=T, channel_multiplier=1))
            pool.sem_inc(s_const, 1)
            pool.wait_ge(s_var, 1)
            pool.tensor_tensor(out=rstd[:, :], in0=rstd[:, :], in1=power[:, :], op=ALU.pow).then_inc(s_rstd, 1)

            def second_rstd(b):
                g = slice(b * GROUP, (b + 1) * GROUP)
                pool.wait_ge(s_var, b + 2)
                pool.tensor_tensor(out=rstd2[:, g], in0=rstd2[:, g], in1=power[:, g], op=ALU.pow).then_inc(s_rstd, 1)

            for b in range(2):
                second_rstd(b)
            for i in range(SUMS):
                pool.dma_start(sums_dram[i].rearrange("(j p) c -> p j c", p=P),
                               pad_rows[:, 0:H].unsqueeze(1).to_broadcast([P, J + 1, H])).then_inc(s_clear, 16)
            for j in range(J):
                pool.wait_ge(s_slot, 1 + [j in js for js in PLACED].index(True))
                for k in range(TOPK):
                    pool.indirect_dma_start(rows_dram[:, :], bass.IndirectOffsetOnAxis(ap=row_i[:, j, k:k + 1], axis=0),
                                            rows[:, j, :], None).then_inc(s_scat, 16)
                    if j == 0 and k in (0, 2):
                        second_rstd(2 + k // 2)
            pool.wait_ge(s_tiles, 1)
            pool.wait_ge(s_clear, 16 * SUMS)

            def turn(i, s, first=False):
                t = i * RING + s
                if not first or s >= SUMS:
                    pool.wait_ge(s_add[(s - SUMS) % RING], 16 * i + (16 if s >= SUMS else 0))
                pool.wait_ge(s_yc, t + (J + 1))
                pool.sem_inc(s_go, 1)
                pool.indirect_dma_start(sums_dram[s % SUMS][:, :], bass.IndirectOffsetOnAxis(ap=idx[:, s:s + 1], axis=0),
                                        y[:, s, :], None, compute_op=ALU.add).then_inc(s_add[s], 16)

            for s in range(RING):
                turn(0, s, first=True)
            last = load_last(pool)
            with pool.Fori(1, FULL) as i:
                with pool.If(i < last + 1):
                    for s in range(RING):
                        turn(i, s)
            for s in range(REST):
                turn(last + 1, s)

        @block.scalar
        def _(act):
            for c in range(2):
                act.dma_start(wij[:, c:c + 1], w_adj[:, c * D:(c + 1) * D].rearrange("o d -> d o")).then_inc(s_wadj, 16)
            act.wait_ge(s_wadj, 32)
            nc.scalar.activation(tg[0:D, :], wij[:, :], ACT.Sigmoid).then_inc(s_table, 1)
            act.wait_ge(s_table, 1)
            for c in range(2):
                act.wait_ge(s_ctxT, c + 1)
                nc.scalar.activation(ctxT[:, c * 512:(c + 1) * 512], pX[c][0:D, :], ACT.Copy).then_inc(s_ctxTc, 1)
            act.wait_ge(s_gates, 48)
            nc.scalar.activation(tg[:, :], gates[:, :], ACT.Tanh).then_inc(s_tanh, 1)
            act.wait_ge(s_sib, 1)

            def sigmoid(j):
                nc.scalar.activation(xs[:, j, :], xs[:, j, :], ACT.Identity, scale=xa[:, j:j + 1],
                                     bias=xc[:, j:j + 1]).then_inc(s_sig, 1)
                if j % HALVES == 0:
                    act.wait_ge(s_sj, j // HALVES + 2)
                if j >= 4:
                    act.wait_ge(s_x1, j - 3)
                nc.scalar.activation(sig[:, j % 4, :], sj_banks[j // HALVES][:, 0:N], ACT.Sigmoid,
                                     bias=sib[:, j:j + 1]).then_inc(s_sig, 1)

            def copy_xnT(b):
                for j in range(b * GROUP, (b + 1) * GROUP):
                    act.wait_ge(s_xnT, j + 1)
                    nc.scalar.activation(xnT[:, :, j * P:(j + 1) * P],
                                         xn_banks[j % 4][:, 0:K * P].rearrange("p (k t) -> p k t", k=K),
                                         ACT.Copy).then_inc(s_xnTc, 1)

            def score(b):
                act.wait_ge(s_logit, b + 1)
                nc.scalar.activation(scoresT[:, :], logit_bank[0:E, 0:GROUP * P], ACT.Sigmoid).then_inc(s_scoreT, 1)

            def copy_score(b):
                act.wait_ge(s_scored, b + 1)
                nc.scalar.activation(scores[:, b * GROUP:(b + 1) * GROUP, :].rearrange("p j e -> p (j e)"),
                                     score_bank[:, 0:GROUP * E], ACT.Copy).then_inc(s_score, 1)

            for j in range(4):
                sigmoid(j)
            copy_xnT(0)
            sigmoid(4)
            score(0)
            sigmoid(5)
            copy_score(0)
            copy_xnT(1)
            sigmoid(6)
            score(1)
            sigmoid(7)
            copy_score(1)
            for b in range(2, B):
                copy_xnT(b)
                score(b)
                copy_score(b)

            def silu(n, par):
                act.wait_ge(s_gu, n + 1)
                nc.scalar.activation(sg[:, par, :], pG[par][:, 0:M], ACT.Silu).then_inc(s_silu, 1)

            for n in range(UNITS):
                silu(n, n % 2)
                first = E - ACT_PADS + 2 * (n - PAD_TURN)
                for e in range(first, min(first + 2, E)) if n >= PAD_TURN else ():
                    act.wait_ge(s_pad_at, 1)
                    at = act.value_load(pad_at[0:1, e:e + 1], min_val=0, max_val=IDLE - P)
                    act.dma_start(rows_dram[bass.ds(at, P), :], pad_rows[:, :]).then_inc(s_pads, 16)

            def copy_xT(t, par):
                act.wait_ge(s_xT, t + 1)
                nc.scalar.activation(xT[:, par, :, :].rearrange("p k t -> p (k t)"), pX[par][:, 0:K * P],
                                     ACT.Copy).then_inc(s_xTc, 1)

            def scale_y(t, s, reused, i):
                act.wait_ge(s_y, t + (J + 1))
                act.wait_ge(s_taken, t + 1)
                if reused:
                    act.wait_ge(s_add[s], i * 16)
                nc.scalar.activation(y[:, s, :], pY[s % 2][:, 0:H], ACT.Copy, scale=wt[:, s:s + 1]).then_inc(s_yc, 1)

            act.wait_ge(s_tiles, 1)
            copy_xT(0, 0)
            copy_xT(1, 1)
            silu(UNITS, 0)

            def turn(i, s, left=RING, before=2):
                t = i * RING + s
                if left > 2:
                    copy_xT(t + 2, s % 2)
                if left > 1:
                    silu(t + (UNITS + 1), (s + 1) % 2)
                if s:
                    scale_y(t - 1, s - 1, before > 0, i)
                elif before:
                    scale_y(t - 1, RING - 1, before > 1, i - 1)

            for i in range(2):
                for s in range(RING):
                    turn(i, s, before=i)
            last = load_last(act)
            with act.Fori(2, FULL - 1) as i:
                with act.If(i < last):
                    for s in range(RING):
                        turn(i, s)
            for n in range(RING + REST):
                turn(last + n // RING, n % RING, RING + REST - n)
            scale_y(last * RING + (RING + REST - 1), REST - 1, True, last + 1)

        @block.tensor
        def _(pe):
            pe.wait_ge(s_const, 1)
            pe.wait_ge(s_ctx, 16)
            for j in range(J):
                ins = nc.tensor.transpose(pX[j // 4][0:D, (j % 4) * P:(j % 4 + 1) * P], ctx_sb[:, j, :], ident[:, :])
                if j % 4 == 3:
                    ins.then_inc(s_ctxT, 1)
            pe.wait_ge(s_wadj, 32)
            pe.wait_ge(s_wide, 1)
            pe.wait_ge(s_ctxTc, 2)
            for j in range(J):
                ins = nc.tensor.matmul(si_bank[:, j:j + 1], ctxT[:, j * P:(j + 1) * P], wij[:, 0:1], start=True, stop=True)
            ins.then_inc(s_sj, 1)
            for b in range(B):
                nc.tensor.matmul(sj_banks[b][:, 0:N], wj_wide[:, :],
                                 ctxT[:, b * N:(b + 1) * N], start=True, stop=True).then_inc(s_sj, 1)

            def router(b):
                for j in range(b * GROUP, (b + 1) * GROUP):
                    pe.wait_ge(s_xn, j + 1)
                    if j >= 4:
                        pe.wait_ge(s_xnTc, j - 3)
                    for k in range(K):
                        ins = nc.tensor.transpose(xn_banks[j % 4][:, k * P:(k + 1) * P], xn[:, j, k * P:(k + 1) * P], ident[:, :])
                    ins.then_inc(s_xnT, 1)
                pe.wait_ge(s_xnTc, (b + 1) * GROUP)
                for k in range(K):
                    ins = nc.tensor.matmul(logit_bank[0:E, 0:GROUP * P], wr[:, k, :],
                                           xnT[:, k, b * GROUP * P:(b + 1) * GROUP * P], start=(k == 0), stop=(k == K - 1))
                ins.then_inc(s_logit, 1)
                pe.wait_ge(s_scoreT, b + 1)
                if b:
                    pe.wait_ge(s_score, b)
                for g in range(GROUP):
                    ins = nc.tensor.transpose(score_bank[:, g * E:(g + 1) * E], scoresT[:, g * P:(g + 1) * P], ident[0:E, 0:E])
                ins.then_inc(s_scored, 1)

            def places(b):
                pe.wait_ge(s_chosen, b + 1)
                js = PLACED[b]
                many = len(js)
                mine = chosen_b[:, js.start:js.stop, :]
                place = pos_banks[b][:, 0:many * E]
                nc.tensor.matmul(place, before[:, :], mine.rearrange("p j e -> p (j e)"), start=True, stop=False)
                for j in range(js.start):
                    nc.tensor.matmul(place.rearrange("p (j e) -> p j e", e=E), ones[:, :],
                                     chosen_b[:, j:j + 1, :].to_broadcast([P, many, E]), start=False, stop=False)
                for d in range(1, many):
                    ins = nc.tensor.matmul(pos_banks[b][:, d * E:many * E], ones[:, :],
                                           mine[:, 0:many - d, :].rearrange("p j e -> p (j e)"),
                                           start=False, stop=(d == many - 1))
                ins.then_inc(s_pos, 1)

            def gate_up(n, par, left, w):
                for k in range(K):
                    ins = nc.tensor.matmul(pG[par][:, 0:2 * M], left(k), w(k), start=(k == 0), stop=(k == K - 1))
                ins.then_inc(s_gu, 1)

            def turn_h(n, par):
                pe.wait_ge(s_h, n + 1)
                nc.tensor.transpose(pH[par][:, 0:P], h[:, par, 0:P], ident[:, :])
                nc.tensor.transpose(pH[par][0:M2, P:2 * P], h[:, par, P:M], ident[:, :]).then_inc(s_hT, 1)

            def down(n, par, bank, w0, w1, start, stop):
                nc.tensor.matmul(bank[:, 0:H], hT[:, par, 0, :], w0, start=start, stop=False)
                ins = nc.tensor.matmul(bank[:, 0:H], hT[0:M2, par, 1, :], w1, start=False, stop=stop)
                if stop:
                    ins.then_inc(s_y, 1)

            def shared_gate_up(n):
                gate_up(n, n % 2, lambda k: xnT[:, k, (n // SH) * P:(n // SH + 1) * P], lambda k: sgu[:, n % SH, k, :])

            def shared_down(n):
                j, part = n // SH, n % SH
                if part == 0 and j >= 2:
                    pe.wait_ge(s_yc, j - 1)
                down(n, n % 2, pY[j % 2], sd0[:, part, :], sd1[:, part, :], part == 0, part == SH - 1)

            def shared_turn(n):
                if n + 1 < UNITS:
                    shared_gate_up(n + 1)
                turn_h(n, n % 2)
                if n:
                    shared_down(n - 1)

            pe.wait_ge(s_wr, 16)
            for b in range(2):
                router(b)
            pe.wait_ge(s_const, 3)
            places(0)
            for b in range(2, B):
                router(b)
            pe.wait_ge(s_shw, 16 * 4 * SH)
            shared_gate_up(0)
            places(1)
            for n in range(3):
                shared_turn(n)
            places(2)
            pe.wait_ge(s_score, B)
            for j in range(J):
                ins = nc.tensor.matmul(count_bank[:, 0:E], ones[:, :], chosen_b[:, j, :], start=(j == 0), stop=(j == J - 1))
            ins.then_inc(s_count, 1)
            for n in range(3, TABLE_TURN):
                shared_turn(n)
            pe.wait_ge(s_tile_of, 1)
            nc.tensor.transpose(table_bank[0:2, 0:P], tile_of[:, :], ident[:, :]).then_inc(s_tableT, 1)
            for n in range(TABLE_TURN, UNITS):
                shared_turn(n)
            pe.wait_ge(s_hTc, UNITS)
            shared_down(UNITS - 1)
            pe.wait_ge(s_tiles, 1)

            def transpose_x(s, rounds, par):
                pe.wait_ge(s_load[s], 16 * rounds)
                for k in range(K):
                    ins = nc.tensor.transpose(pX[par][:, k * P:(k + 1) * P], xg[:, s, k * P:(k + 1) * P], ident[:, :])
                ins.then_inc(s_xT, 1)

            def routed_gate_up(t, par, e):
                pe.wait_ge(s_xTc, t + 1)
                gate_up(None, par, lambda k: xT[:, par, k, :], lambda k: wgu[:, bass.ds(e, 1), k, :])

            pe.wait_ge(s_expw[0], 16 * FIRST)

            def look_up(t):
                return pe.value_load(tiles[0:1, bass.ds(t, 1)], min_val=0, max_val=E - 1)

            transpose_x(0, 1, 0)
            transpose_x(1, 1, 1)
            e_first = look_up(0)
            routed_gate_up(0, 0, e_first)

            def routed_down(t, par, e):
                down(t + UNITS, par, pY[par], wd0[:, bass.ds(e, 1), :], wd1[:, bass.ds(e, 1), :], True, True)

            def iteration(i, first=False, tiles=None):
                e = e_next = None
                for s in range(tiles or RING):
                    left = tiles - s if tiles else RING
                    t = i * RING + s
                    e_before, e = e, e_next
                    if left > 2:
                        transpose_x((s + 2) % RING, i + (s + 2) // RING + 1, s % 2)
                    if left > 1:
                        e_next = look_up(t + 1)
                        routed_gate_up(t + 1, (s + 1) % 2, e_next)
                    if s == 0 and not first:
                        e_before = look_up(t - 1)
                    if s == 1:
                        e_before = look_up(t - 1)
                    turn_h(t + UNITS, s % 2)
                    if e_before is not None:
                        routed_down(t - 1, (s + 1) % 2, e_before)
                return e

            early = (FIRST - 1) // RING
            iteration(0, first=True)
            with pe.Fori(1, early) as i:
                iteration(i)
            pe.wait_ge(s_expw[1], 16 * (E - FIRST))
            last = load_last(pe)
            with pe.Fori(early, FULL - 1) as i:
                with pe.If(i < last):
                    iteration(i)
            e_last = iteration(last, tiles=RING + REST)
            pe.wait_ge(s_hTc, last * RING + (RING + REST + UNITS))
            pe.wait_ge(s_yc, last * RING + (RING + REST - 2 + J))
            routed_down(last * RING + (RING + REST - 1), (REST - 1) % 2, e_last)

        @block.vector
        def _(dve):
            made = [0]
            V = nc.vector

            def link(ins):
                made[0] += 1
                ins.then_inc(s_dve, 1)
                dve.wait_ge(s_dve, made[0])

            V.memset(gkey[:, :, :], ABSENT)
            V.memset(key[:, :, :], ABSENT)
            V.memset(zero_e[:, :], 0.0)
            dve.wait_ge(s_wadj, 32)
            V.tensor_copy(wj_wide[:, :], wij[:, 1:2].to_broadcast([D, P])).then_inc(s_wide, 1)

            for j in range(J):
                if j % HALVES == 0:
                    dve.wait_ge(s_xin[j // HALVES], 16)
                ins = V.bn_stats(stats[:, j, :], xs[:, j, :])
            link(ins)
            for j in range(J):
                ins = V.bn_aggr(mv[:, j, :], stats[:, j, :])
            link(ins)
            V.tensor_scalar(rstd[:, :], mv[:, :, 1], EPS, None, ALU.add).then_inc(s_var, 1)
            dve.wait_ge(s_tanh, 1)
            V.tensor_scalar(kx[:, 0:1], tg[:, 0:1], 1.0 - P_ASEM, None, ALU.mult)
            link(V.tensor_scalar(kx[:, 1:2], tg[:, 0:1], P_ASEM, None, ALU.mult))
            dve.wait_ge(s_rstd, 1)
            link(V.tensor_scalar(xa[:, :], rstd[:, :], kx[:, 0:1], None, ALU.mult))
            link(V.scalar_tensor_tensor(xc[:, :], mv[:, :, 0], -1.0, xa[:, :], op0=ALU.mult, op1=ALU.mult))
            link(V.tensor_scalar(xa[:, :], xa[:, :], 1.0, None, ALU.add))
            dve.wait_ge(s_gates, 48)
            dve.wait_ge(s_sj, 1)
            V.tensor_scalar(sib[:, :], si_bank[:, 0:J], badj[:, 0:1], None, ALU.add).then_inc(s_sib, 1)

            def norm_group(b):
                dve.wait_ge(s_rstd, b + 2)
                for j in range(b * GROUP, (b + 1) * GROUP):
                    V.tensor_scalar(xn[:, j, :], xs[:, j, :], mv[:, j, 0:1], rstd2[:, j:j + 1],
                                    ALU.subtract, ALU.mult).then_inc(s_xn, 1)

            def mix_group(b):
                for j in range(b * GROUP, (b + 1) * GROUP):
                    dve.wait_ge(s_sig, 2 * j + 2)
                    V.scalar_tensor_tensor(xs[:, j, :], sig[:, j % 4, :], kx[:, 1:2], xs[:, j, :],
                                           op0=ALU.mult, op1=ALU.add).then_inc(s_x1, 1)

            def measure_group(b):
                js = range(b * GROUP, (b + 1) * GROUP)
                dve.wait_ge(s_x1, js.stop)
                for j in js:
                    ins = V.bn_stats(stats[:, j, :], xs[:, j, :])
                link(ins)
                for j in js:
                    ins = V.bn_aggr(mv[:, j, :], stats[:, j, :])
                link(ins)
                V.tensor_scalar(rstd2[:, js.start:js.stop], mv[:, js.start:js.stop, 1], EPS, None, ALU.add).then_inc(s_var, 1)

            mix_group(0)
            measure_group(0)
            mix_group(1)
            norm_group(0)
            measure_group(1)
            norm_group(1)

            dve.wait_ge(s_cb, 16)
            dve.wait_ge(s_const, 4)

            def choose(js, marks, keys, n, top):
                for j in js:
                    ins = V.max(best[:, j, :], keys[:, j, 0:n])
                link(ins)
                link(V.memset(best[:, js.start:js.stop, top:8], ABSENT))
                for j in js:
                    ins = V.match_replace(out=marks[:, j, :], in_to_replace=best[:, j, :], in_values=keys[:, j, :],
                                          imm_value=CHOSEN)
                link(ins)

            def choose_groups(b):
                js = PLACED[b]
                many = len(js)
                g = slice(js.start, js.stop)
                dve.wait_ge(s_score, js.stop // GROUP)
                link(V.tensor_tensor(sfc[:, g, :], scores[:, g, :],
                                     cb[:, :].unsqueeze(1).to_broadcast([P, many, E]), ALU.add))
                four = sfc[:, g, :].rearrange("p j (g e) -> p j g e", e=PER)
                a, c, d, f = (pair[:, i, g.start * GROUPS:g.stop * GROUPS].rearrange("p (j g) -> p j g", g=GROUPS)
                              for i in range(4))
                V.tensor_tensor(a, four[:, :, :, 0], four[:, :, :, 1], ALU.max)
                V.tensor_tensor(c, four[:, :, :, 0], four[:, :, :, 1], ALU.min)
                V.tensor_tensor(d, four[:, :, :, 2], four[:, :, :, 3], ALU.max)
                link(V.tensor_tensor(f, four[:, :, :, 2], four[:, :, :, 3], ALU.min))
                link(V.tensor_tensor(c, c, f, ALU.max))
                link(V.tensor_tensor(f, a, d, ALU.min))
                V.tensor_tensor(a, a, d, ALU.max)
                link(V.tensor_tensor(c, c, f, ALU.max))
                link(V.tensor_tensor(gkey[:, g, 0:GROUPS], a, c, ALU.add))
                choose(js, gmark, gkey, GROUPS, TOPK_GROUPS)

            def choose_experts(b):
                js = PLACED[b]
                g = slice(js.start, js.stop)
                link(V.tensor_scalar(gmark[:, g, 0:GROUPS], gmark[:, g, 0:GROUPS], CHOSEN, BARRED, ALU.is_lt, ALU.mult))
                for j in js:
                    ins = V.tensor_tensor(key[:, j, 0:E].rearrange("p (g e) -> p g e", e=PER),
                                          sfc[:, j, :].rearrange("p (g e) -> p g e", e=PER),
                                          gmark[:, j, 0:GROUPS].unsqueeze(2).to_broadcast([P, GROUPS, PER]), ALU.add)
                link(ins)
                choose(js, mark, key, E, TOPK)
                V.tensor_scalar(chosen_b[:, g, :], mark[:, g, 0:E], CHOSEN, None, ALU.is_equal).then_inc(s_chosen, 1)
                link(V.tensor_scalar(chosen[:, g, :], mark[:, g, 0:E], CHOSEN, None, ALU.is_equal))
                V.scalar_tensor_tensor(comb[:, g, :], scores[:, g, :], tg[:, 1:2], chosen[:, g, :],
                                       op0=ALU.mult, op1=ALU.mult)

            def choose_rows(b):
                js = PLACED[b]
                many = len(js)
                g = slice(js.start, js.stop)
                dve.wait_ge(s_pos, b + 1)
                link(V.tensor_tensor(mark[:, g, 0:E], pos_banks[b][:, 0:many * E].rearrange("p (j e) -> p j e", e=E),
                                     region[:, :].unsqueeze(1).to_broadcast([P, many, E]), ALU.add))
                link(V.tensor_tensor(mark[:, g, 0:E], mark[:, g, 0:E], chosen[:, g, :], ALU.mult))
                for j in js:
                    ins = V.max(best[:, j, :], mark[:, j, 0:E])
                link(ins)
                V.tensor_scalar(row_i[:, g, :], best[:, g, :], -1.0, None, ALU.add).then_inc(s_slot, 1)

            def gate(n, par):
                dve.wait_ge(s_silu, n + 1)
                V.tensor_tensor(h[:, par, :], sg[:, par, :], pG[par][:, M:2 * M], ALU.mult).then_inc(s_h, 1)

            def copy_hT(n, par):
                dve.wait_ge(s_hT, n + 1)
                V.tensor_copy(hT[:, par, 0, :], pH[par][:, 0:P])
                V.tensor_copy(hT[0:M2, par, 1, :], pH[par][0:M2, P:2 * P]).then_inc(s_hTc, 1)

            def shared_out(j):
                dve.wait_ge(s_y, j + 1)
                V.scalar_tensor_tensor(xs[:, j, :], pY[j % 2][:, 0:H], tg[:, 1:2], xs[:, j, :],
                                       op0=ALU.mult, op1=ALU.add).then_inc(s_yc, 1)

            def shared_turn(n):
                copy_hT(n, n % 2)
                if n + 1 < UNITS:
                    gate(n + 1, (n + 1) % 2)
                if n >= SH + 1 and (n - 1) % SH == 0:
                    shared_out((n - 1) // SH - 1)

            choose_groups(0)
            choose_experts(0)
            mix_group(2)
            choose_rows(0)
            measure_group(2)
            norm_group(2)
            mix_group(3)
            measure_group(3)
            norm_group(3)
            choose_groups(1)
            choose_experts(1)
            choose_rows(1)
            gate(0, 0)
            shared_turn(0)
            choose_groups(2)
            shared_turn(1)
            choose_experts(2)
            shared_turn(2)
            choose_rows(2)

            dve.wait_ge(s_count, 1)
            link(V.tensor_copy(ntile[:, :], count_bank[:, 0:E]))
            V.scalar_tensor_tensor(pad_at[0:1, :], ntile[0:1, :], -1.0, region[0:1, :],
                                   op0=ALU.add, op1=ALU.add).then_inc(s_pad_at, 1)
            for n in range(3, TABLE_TURN - 2):
                shared_turn(n)

            link(V.tensor_scalar(cnt_i[:, 0, :], ntile[:, :], float(P - 1), None, ALU.add))
            link(V.tensor_scalar(cnt_i[:, 1, :], cnt_i[:, 0, :], P.bit_length() - 1, None, ALU.logical_shift_right))
            link(V.tensor_scalar(ntile[:, :], cnt_i[:, 1, :], 1.0, None, ALU.max))
            link(V.tensor_tensor_scan(tend[:, :], ntile[:, :], zero_e[:, :], 0.0, ALU.add, ALU.add))
            link(V.tensor_scalar(round_is[:, :], round_ends[:, :], tend[0:1, E - 1:E], None, ALU.is_lt))
            link(V.reduce_sum(last_f[:, :], round_is[:, :], axis=mybir.AxisListType.X))
            V.tensor_copy(last_i[:, :], last_f[:, :])
            link(V.tensor_tensor(tbase[:, :], tend[:, :], ntile[:, :], ALU.subtract))
            shared_turn(TABLE_TURN - 2)
            link(V.tensor_scalar(past[:, :], tend[:, :], part_f[:, 0:1], None, ALU.is_le))
            link(V.tensor_scalar(cur[:, :], tbase[:, :], part_f[:, 0:1], None, ALU.is_le))
            link(V.tensor_tensor(cur[:, :], cur[:, :], past[:, :], ALU.subtract))
            link(V.reduce_sum(used[:, :], cur[:, :], axis=mybir.AxisListType.X))
            link(V.reduce_sum(tile_of[:, 0:1], past[:, :], axis=mybir.AxisListType.X))
            link(V.tensor_scalar(tile_of[:, 0:1], tile_of[:, 0:1], float(E - 1), None, ALU.min))
            link(V.scalar_tensor_tensor(tbase[:, :], tbase[:, :], -float(P), region[:, :], op0=ALU.mult, op1=ALU.add))
            link(V.tensor_tensor(cur[:, :], cur[:, :], tbase[:, :], ALU.mult))
            link(V.reduce_sum(tile_of[:, 1:2], cur[:, :], axis=mybir.AxisListType.X))
            link(V.tensor_scalar(part_f[:, :], part_f[:, :], float(P), -float(IDLE + 1), ALU.mult, ALU.add))
            link(V.scalar_tensor_tensor(tile_of[:, 1:2], used[:, :], part_f[:, 0:1], tile_of[:, 1:2],
                                        op0=ALU.mult, op1=ALU.add))
            V.tensor_scalar(tile_of[:, 1:2], tile_of[:, 1:2], float(IDLE), None, ALU.add).then_inc(s_tile_of, 1)
            for n in range(TABLE_TURN - 1, TABLE_TURN + 1):
                shared_turn(n)
            dve.wait_ge(s_tableT, 1)
            V.tensor_copy(tiles[:, :], table_bank[0:2, 0:P]).then_inc(s_tiles, 1)
            dve.wait_ge(s_tiles, 1)
            for n in range(TABLE_TURN + 1, UNITS):
                shared_turn(n)
            shared_out(J - 1)

            def take(t, s, rounds, used=True):
                e = dve.value_load(tiles[0:1, bass.ds(t, 1)], min_val=0, max_val=E - 1)
                dve.wait_ge(s_load[s], 16 * rounds)
                V.tensor_copy(wt[:, s:s + 1], xg[:, s, bass.ds(e + H, 1)])
                if used:
                    dve.wait_ge(s_add[s], 16 * rounds - 16)
                V.tensor_copy(idx[:, s:s + 1], xg[:, s, H + E:ROW].bitcast(I32)).then_inc(s_taken, 1)

            take(0, 0, 1, used=False)
            gate(UNITS, 0)

            def turn(i, s, left=RING, first=False):
                t = i * RING + s
                copy_hT(t + UNITS, s % 2)
                if left > 1:
                    gate(t + (UNITS + 1), (s + 1) % 2)
                if left > 1:
                    take(t + 1, (s + 1) % RING, i + (s + 1) // RING + 1, used=not first or s + 1 >= RING)

            for s in range(RING):
                turn(0, s, first=True)
            last = load_last(dve)
            with dve.Fori(1, FULL - 1) as i:
                with dve.If(i < last):
                    for s in range(RING):
                        turn(i, s)
            for n in range(RING + REST):
                turn(last + n // RING, n % RING, RING + REST - n)
            for i, routed in ends:
                for b in range(B):
                    js = slice(b * HALVES, (b + 1) * HALVES)
                    dve.wait_ge(s_sums[i][b], 16)
                    ins = V.tensor_tensor(xs[:, js, :], xs[:, js, :], routed[:, js, :], ALU.add)
                    if i == LAST_SUM:
                        ins.then_inc(s_fin, 1)
                if i != LAST_SUM:
                    link(ins)


_INS = ['x', 'ctx_512', 'g_xattn', 'g_ffn', 'L0_xattn_W', 'L0_xattn_b', 'L0_ffn_w_router', 'L0_ffn_corr_bias',
        'L0_ffn_gate_w', 'L0_ffn_up_w', 'L0_ffn_down_w', 'L0_ffn_sh_gate_w', 'L0_ffn_sh_up_w', 'L0_ffn_sh_down_w']
_OUTS = [((4, 256, 256), 'float32')]


def kernel(**inputs):
    import numpy as _np
    import concourse.bacc as _bacc
    from concourse import mybir as _mybir
    from concourse.bass_utils import run_bass_kernel_spmd as _run

    nc = _bacc.Bacc("TRN2", target_bir_lowering=False, num_devices=1)
    arrays, args = {}, []
    for name in _INS:
        a = _np.ascontiguousarray(inputs[name])
        arrays[f"in_{name}_dram"] = a
        args.append(nc.dram_tensor(f"in_{name}_dram", a.shape, _mybir.dt.from_np(a.dtype), kind="ExternalInput").ap())
    for i, (shape, dtype) in enumerate(_OUTS):
        dt = _mybir.dt.from_np(_np.dtype(dtype))
        args.append(nc.dram_tensor(f"out_{i}_dram", shape, dt, kind="ExternalOutput").ap())
    gated_xattn_moe(nc, *args)
    r = _run(nc, [arrays], core_ids=[0])
    got = tuple(r.results[0][f"out_{i}_dram"] for i in range(len(_OUTS)))
    return got[0]
```
